# Optimizing a Trainium2 kernel written in Bass

```python
import numpy as np
import jax
import jax.numpy as jnp

def _softmax(x, axis=-1):
    return jax.nn.softmax(x, axis=axis)

def _gelu(x):
    return jax.nn.gelu(x, approximate=True)

def _silu(x):
    return jax.nn.silu(x)

def _sigmoid(x):
    return jax.nn.sigmoid(x)

def _layernorm(x, axis=-1, eps=1e-05):
    m = jnp.mean(x, axis=axis, keepdims=True)
    v = jnp.var(x, axis=axis, keepdims=True)
    return (x - m) / jnp.sqrt(v + eps)

def _scatter_add(tgt, idx, src, axis=0):
    return tgt.at[idx].add(src)

def _segment_sum(src, seg, n):
    return jax.ops.segment_sum(src, seg, n)
kernel_name = 'mk_prb_d1_jaxref_r8_51bd08'

def setup_inputs(seed: int=0):
    np.random.seed(seed)
    _w = jnp.asarray

    def _L0_attn_setup():
        import jax, jax.numpy as jnp
        import numpy as np
        D_MODEL = 128
        N_HEADS = 16
        D_HEAD = D_MODEL // N_HEADS
        B, T = (2, 256)
        EPS = 1e-05
        key = jax.random.key(seed)
        ks = jax.random.split(key, 5)
        s = 1.0 / np.sqrt(D_MODEL)
        return {'x': jax.random.normal(ks[0], (B, T, D_MODEL), dtype=jnp.float32), 'W_q': jax.random.normal(ks[1], (D_MODEL, D_MODEL), dtype=jnp.float32) * s, 'W_k': jax.random.normal(ks[2], (D_MODEL, D_MODEL), dtype=jnp.float32) * s, 'W_v': jax.random.normal(ks[3], (D_MODEL, D_MODEL), dtype=jnp.float32) * s, 'W_o': jax.random.normal(ks[4], (D_MODEL, D_MODEL), dtype=jnp.float32) * s, 'gn_weight': jnp.ones((D_MODEL,), dtype=jnp.float32), 'gn_bias': jnp.zeros((D_MODEL,), dtype=jnp.float32)}
    _L0_attn_in = _L0_attn_setup()

    def _L0_ffn_setup():
        import jax, jax.numpy as jnp
        import numpy as np
        LOOPS = 2
        NUM_GROUPS = 4
        EXPERTS_PER_GROUP = 2
        NUM_EXPERTS = NUM_GROUPS * EXPERTS_PER_GROUP
        GROUPS_TOP_K = 2
        TOP_K = 1
        RMS_EPS = 1e-06
        EPS = 1e-09

        def _rmsnorm(x, w):
            return x * jax.lax.rsqrt(jnp.mean(x * x, axis=-1, keepdims=True) + RMS_EPS) * w

        def _combine_weights(x_flat, w_macro, w_micro):
            T = x_flat.shape[0]
            macro = jax.nn.softmax(x_flat @ w_macro.T, axis=-1)
            mvals, midx = jax.lax.top_k(macro, GROUPS_TOP_K)
            mvals = mvals / (jnp.sum(mvals, axis=-1, keepdims=True) + EPS)
            micro = jax.nn.softmax(jnp.einsum('td,ged->tge', x_flat, w_micro), axis=-1)
            uvals, uidx = jax.lax.top_k(micro, TOP_K)
            uvals = uvals / (jnp.sum(uvals, axis=-1, keepdims=True) + EPS)
            tok = jnp.arange(T)
            combine = jnp.zeros((T, NUM_EXPERTS), x_flat.dtype)
            for s in range(GROUPS_TOP_K):
                g = midx[:, s]
                wg = mvals[:, s:s + 1]
                li = uidx[tok, g]
                lv = uvals[tok, g]
                eidx = g[:, None] * EXPERTS_PER_GROUP + li
                combine = combine.at[tok[:, None], eidx].add(lv * wg)
            return combine
        key = jax.random.key(seed)
        ks = jax.random.split(key, 6)
        B, S, D, F = (2, 128, 128, 256)
        return {'z': jax.random.normal(ks[0], (B, S, D), jnp.float32), 'norm_w': jnp.ones((D,), jnp.float32), 'w_macro': jax.random.normal(ks[1], (NUM_GROUPS, D), jnp.float32) * D ** (-0.5), 'w_micro': jax.random.normal(ks[2], (NUM_GROUPS, EXPERTS_PER_GROUP, D), jnp.float32) * D ** (-0.5), 'w1': jax.random.normal(ks[3], (NUM_EXPERTS, F, D), jnp.float32) * D ** (-0.5), 'w2': jax.random.normal(ks[4], (NUM_EXPERTS, D, F), jnp.float32) * F ** (-0.5)}
    _L0_ffn_in = _L0_ffn_setup()
    _d = {'L0_attn_x': _L0_attn_in['x'], 'L0_attn_W_q': _L0_attn_in['W_q'], 'L0_attn_W_k': _L0_attn_in['W_k'], 'L0_attn_W_v': _L0_attn_in['W_v'], 'L0_attn_W_o': _L0_attn_in['W_o'], 'L0_attn_gn_weight': _L0_attn_in['gn_weight'], 'L0_attn_gn_bias': _L0_attn_in['gn_bias'], 'L0_ffn_norm_w': _L0_ffn_in['norm_w'], 'L0_ffn_w_macro': _L0_ffn_in['w_macro'], 'L0_ffn_w_micro': _L0_ffn_in['w_micro'], 'L0_ffn_w1': _L0_ffn_in['w1'], 'L0_ffn_w2': _L0_ffn_in['w2']}
    _x0 = _d['L0_attn_x']
    _d['L0_attn_x'] = jax.random.normal(jax.random.fold_in(jax.random.key(seed), 1), (16, 256, 128), dtype=_x0.dtype)
    del _x0
    return _d

def reference(L0_attn_x, L0_attn_W_q, L0_attn_W_k, L0_attn_W_v, L0_attn_W_o, L0_attn_gn_weight, L0_attn_gn_bias, L0_ffn_norm_w, L0_ffn_w_macro, L0_ffn_w_micro, L0_ffn_w1, L0_ffn_w2):

    def _L0_attn_ref(x, W_q, W_k, W_v, W_o, gn_weight, gn_bias):
        import jax, jax.numpy as jnp
        import numpy as np
        D_MODEL = 128
        N_HEADS = 16
        D_HEAD = D_MODEL // N_HEADS
        B, T = (2, 256)
        EPS = 1e-05
        b, t, dm = x.shape
        h, dh = (N_HEADS, D_HEAD)
        gammas = 1.0 - 2.0 ** (-5.0 - jnp.arange(h, dtype=jnp.float32))
        q = (x @ W_q.T).reshape(b, t, h, dh)
        k = (x @ W_k.T).reshape(b, t, h, dh)
        v = (x @ W_v.T).reshape(b, t, h, dh)
        idx = jnp.arange(t)
        diff = idx[:, None] - idx[None, :]
        pow_ = jnp.maximum(diff, 0).astype(jnp.float32)
        decay = jnp.where(diff >= 0, gammas[:, None, None] ** pow_, 0.0)
        scale = jnp.sqrt(jnp.float32(dh))
        attn = jnp.einsum('bihd,bjhd->bhij', q, k) * decay[None] / scale
        y = jnp.einsum('bhij,bjhd->bihd', attn, v)
        mean = y.mean(axis=(1, 3), keepdims=True)
        var = y.var(axis=(1, 3), keepdims=True)
        yn = (y - mean) / jnp.sqrt(var + EPS)
        yn = yn.reshape(b, t, dm) * gn_weight + gn_bias
        return yn @ W_o.T

    def _L0_ffn_ref(z, norm_w, w_macro, w_micro, w1, w2):
        import jax, jax.numpy as jnp
        import numpy as np
        LOOPS = 2
        NUM_GROUPS = 4
        EXPERTS_PER_GROUP = 2
        NUM_EXPERTS = NUM_GROUPS * EXPERTS_PER_GROUP
        GROUPS_TOP_K = 2
        TOP_K = 1
        RMS_EPS = 1e-06
        EPS = 1e-09

        def _rmsnorm(x, w):
            return x * jax.lax.rsqrt(jnp.mean(x * x, axis=-1, keepdims=True) + RMS_EPS) * w

        def _combine_weights(x_flat, w_macro, w_micro):
            T = x_flat.shape[0]
            macro = jax.nn.softmax(x_flat @ w_macro.T, axis=-1)
            mvals, midx = jax.lax.top_k(macro, GROUPS_TOP_K)
            mvals = mvals / (jnp.sum(mvals, axis=-1, keepdims=True) + EPS)
            micro = jax.nn.softmax(jnp.einsum('td,ged->tge', x_flat, w_micro), axis=-1)
            uvals, uidx = jax.lax.top_k(micro, TOP_K)
            uvals = uvals / (jnp.sum(uvals, axis=-1, keepdims=True) + EPS)
            tok = jnp.arange(T)
            combine = jnp.zeros((T, NUM_EXPERTS), x_flat.dtype)
            for s in range(GROUPS_TOP_K):
                g = midx[:, s]
                wg = mvals[:, s:s + 1]
                li = uidx[tok, g]
                lv = uvals[tok, g]
                eidx = g[:, None] * EXPERTS_PER_GROUP + li
                combine = combine.at[tok[:, None], eidx].add(lv * wg)
            return combine
        B, S, D = z.shape
        T = B * S
        for _ in range(LOOPS):
            zn = _rmsnorm(z, norm_w)
            x = zn.reshape(T, D)
            combine = _combine_weights(x, w_macro, w_micro)
            h = jax.nn.silu(jnp.einsum('td,efd->tef', x, w1))
            y = jnp.einsum('tef,edf->ted', h, w2)
            mixed = jnp.einsum('ted,te->td', y, combine)
            z = z + mixed.reshape(B, S, D)
        return z
    x = L0_attn_x
    xn = _layernorm(x, axis=-1)
    x = x + _L0_attn_ref(xn, L0_attn_W_q, L0_attn_W_k, L0_attn_W_v, L0_attn_W_o, L0_attn_gn_weight, L0_attn_gn_bias) + _L0_ffn_ref(xn, L0_ffn_norm_w, L0_ffn_w_macro, L0_ffn_w_micro, L0_ffn_w1, L0_ffn_w2)
    return x

_drawn_inputs = setup_inputs


def setup_inputs(seed=0):
    import zlib

    import numpy as np

    out = dict(_drawn_inputs(seed))
    spreads = {'L0_attn_gn_weight': (1.0, 0.2),
     'L0_attn_gn_bias': (0.0, 0.1),
     'L0_ffn_norm_w': (1.0, 0.2)}
    factors = {}
    for name, (base, spread) in spreads.items():
        noise = np.random.default_rng([zlib.crc32(name.encode()), seed]).standard_normal(out[name].shape)
        drawn = base * np.exp(spread * noise) if base else spread * noise
        out[name] = jnp.asarray(drawn.astype(out[name].dtype))
    for name, factor in factors.items():
        out[name] = (out[name] * factor).astype(out[name].dtype)
    return out
```

```python
from contextlib import ExitStack

import concourse.bass as bass
from concourse import mybir

F32 = mybir.dt.float32
F32R = mybir.dt.float32r
ALU = mybir.AluOpType
ACT = mybir.ActivationFunctionType
AX_X = mybir.AxisListType.X

P = 128
B, T, D = 16, 256, 128
H = 16
DH = D // H
GH = 4
G = H // GH
TB = T // P
ITEM = 512
TI = ITEM // P
NI = B * T // ITEM
SLOTS = 2 * NI
E = 8
NG, PG = 4, 2
F = 256
FC = F // P
K = E * FC
LAG = 3
RING = 4
NR = NG + E
LN_EPS = 1e-5
RMS_EPS = 1e-6
TOPK_EPS = 1e-9
LNC = 4
LNT = B * T // P // LNC

CONST = {}
_at = 0
for _name, _w in (("ident", P), ("causal", P), ("headmask", P), ("headmean", P), ("kdecay_tok", P),
                  ("kdecay", T), ("qdecay", GH * T), ("qdecay_plain", P),
                  ("earlier", NG * NG), ("wins_needed", NG), ("minus_half", 64)):
    CONST[_name] = (_at, _at + _w)
    _at += _w
NCONST = _at

ROUTER_OPS = 24
V_COPIES = 3
QK_OPS = 3
GN_OPS = 10


def constants():
    import numpy as np

    c = np.zeros((P, NCONST), np.float32)

    def put(name, a):
        lo, hi = CONST[name]
        c[:, lo:hi] = np.asarray(a, np.float64).reshape(a.shape[0], -1)

    head = np.arange(P) // DH
    gamma = 1.0 - 2.0 ** (-5.0 - np.arange(H))
    g = gamma[head][:, None]
    t = np.arange(T)[None, :]
    put("ident", np.eye(P))
    put("causal", np.triu(np.ones((P, P))))
    same = (head[:, None] == head[None, :]).astype(float)
    put("headmask", same)
    put("headmean", same / DH)
    put("kdecay_tok", (g ** -np.arange(P)[None, :]).T)
    put("kdecay", g ** -t)
    q = g ** t / np.sqrt(DH)
    mask = ((head % GH)[:, None, None] == np.arange(GH)[None, :, None]).astype(float)
    put("qdecay", mask * q[:, None, :])
    put("qdecay_plain", q[:, P:T])
    put("earlier", np.tile((np.arange(NG)[:, None] > np.arange(NG)[None, :]).astype(float)[None], (P, 1, 1)))
    put("wins_needed", np.tile(np.arange(NG)[None] - 1.0, (P, 1)))
    put("minus_half", np.full((P, 64), -0.5))
    return c


def at(i, per_slot, nth):
    return i * per_slot + nth


def wait(eng, sem, value):
    if isinstance(value, int) and value <= 0:
        return
    eng.wait_ge(sem, value)


def program(nc, x, w_q, w_k, w_v, w_o, gn_weight, gn_bias, norm_w, w_macro, w_micro, w1, w2, const, out):
    z_dram = nc.dram_tensor("z_rounds", (2 * NI * ITEM, D), F32, kind="Internal").ap()
    xa_dram = nc.dram_tensor("x_plus_attn", (B * T, D), F32, kind="Internal").ap()
    c_dram = nc.dram_tensor("combine", (SLOTS * E * TI, P), F32, kind="Internal").ap()
    x_rows = x.rearrange("b t d -> (b t) d")
    out_rows = out.rearrange("b t d -> (b t) d")

    def item_rows(rows, i):
        return rows[bass.ds(i * ITEM, ITEM), :].rearrange("(t p) d -> p t d", p=P)

    def batch_rows(rows, b):
        return rows[bass.ds(b * T, T), :].rearrange("(t p) d -> p t d", p=P)

    with ExitStack() as ctx:
        def sb(name, shape, dt=F32):
            return ctx.enter_context(nc.sbuf_tensor(name, shape, dt))

        def bank(name):
            return ctx.enter_context(nc.psum_tensor(name, [P, 512], F32))

        def sem(name):
            return ctx.enter_context(nc.semaphore(name))

        cst = sb("cst", [P, NCONST])

        def const_of(name):
            return cst[:, CONST[name][0]:CONST[name][1]]

        ident = const_of("ident")
        vecs = sb("vecs", [P, 3])
        norm_col, gnw_col, gnb_col = (vecs[:, n:n + 1] for n in range(3))
        wnat = sb("wnat", [P, 4, D])
        rnat = sb("rnat", [NR, D])
        wT = sb("wT", [P, 4, D])
        rhi = sb("rhi", [P, NR], F32R)
        rlo = sb("rlo", [P, NR], F32R)
        w1hi = sb("w1hi", [P, K, P], F32R)
        w1lo = sb("w1lo", [P, K, P], F32R)
        w2hi = sb("w2hi", [P, K, P], F32R)
        w2lo = sb("w2lo", [P, K, P], F32R)
        xall = sb("xall", [P, LNC, LNT, D])
        w1nat = sb("w1nat", [P, K, D])
        w2nat_sb = sb("w2nat", [P, E, F])
        w2nat = w2nat_sb[:]

        def w2nat_block(c):
            return w2nat_sb[:, c // FC, (c % FC) * P:(c % FC + 1) * P]

        stats = sb("stats", [P, LNC, LNT, 6])
        ln = sb("ln", [P, LNC, 6, LNT])
        zt = sb("zt", [P, TI, D])
        zn = sb("zn", [P, TI, D])
        ms = sb("ms", [P, 2, TI])
        rstd = sb("rstd", [P, TI])
        zhi = sb("zhi", [P, 2, ITEM], F32R)
        zlo = sb("zlo", [P, 2, ITEM], F32R)
        logit = sb("logit", [P, TI, NR])
        rt = sb("rt", [P, 24, TI * NG])
        beats = sb("beats", [P, 3, TI, NG, NG])
        combine = sb("combine_tok", [P, NG, PG, TI])
        combine_T = sb("combine_T", [E * TI, P])
        cbc = sb("cbc", [P, 2, E, ITEM])
        hf = sb("hf", [P, RING, ITEM])
        hhi = sb("hhi", [P, RING, ITEM], F32R)
        hlo = sb("hlo", [P, RING, ITEM], F32R)
        prod = sb("prod", [P, 2, ITEM])
        acc = sb("acc", [P, 2, ITEM])
        base = sb("base", [P, TI, D])
        xa_in = sb("xa_in", [P, TI, D])
        res = sb("res", [P, TI, D])
        xt = sb("xt", [P, TB, D])
        xres = sb("xres", [P, TB, D])
        xT = sb("xT", [P, T])
        qblk = sb("qblk", [P, GH, T])
        q1 = sb("q1", [P, P])
        kT = sb("kT", [P, T])
        vpad = sb("vpad", [P, TB, G, GH, GH, DH])
        v0 = sb("v0", [P, P])
        k0 = sb("k0", [P, P])
        state = sb("state", [P, P])
        A = sb("A", [P, TB, G, GH, P])
        gst = sb("gst", [P, 6])
        gsq = sb("gsq", [P, 3])
        gmv = sb("gmv", [P, 2])
        ghm = sb("ghm", [P, 2])
        gv = sb("gv", [P, 4])
        ynT = sb("ynT", [P, T])
        xa_out = sb("xa_out", [P, TB, D])

        up = [bank(f"up{n}") for n in range(2)]
        down = [bank(f"down{n}") for n in range(2)]
        m0, m1, pp, yy = bank("m0"), bank("m1"), bank("pp"), bank("yy")

        s_const = sem("s_const")
        s_vecs = sem("s_vecs")
        s_wnat = sem("s_wnat")
        s_rnat = sem("s_rnat")
        s_w1nat = sem("s_w1nat")
        s_w2nat = sem("s_w2nat")
        s_xall = [sem(f"s_xall{n}") for n in range(LNC)]
        s_zt = sem("s_zt")
        s_xt = sem("s_xt")
        s_xres = sem("s_xres")
        s_base = sem("s_base")
        s_xa_in = sem("s_xa_in")
        s_cbc = sem("s_cbc")
        s_z_stored = sem("s_z_stored")
        s_xa_stored = sem("s_xa_stored")
        s_c_stored = sem("s_c_stored")
        s_wtp = sem("s_wtp")
        s_whi = sem("s_whi")
        s_wlo = sem("s_wlo")
        s_ln = sem("s_ln")
        s_ln_chain = sem("s_ln_chain")
        s_ln_var = sem("s_ln_var")
        s_ln_pow = sem("s_ln_pow")
        s_sq = sem("s_sq")
        s_ms = sem("s_ms")
        s_rstd = sem("s_rstd")
        s_zn = sem("s_zn")
        s_zT = sem("s_zT")
        s_zhi = sem("s_zhi")
        s_zlo = sem("s_zlo")
        s_logit = sem("s_logit")
        s_logit_sb = sem("s_logit_sb")
        s_router = sem("s_router")
        s_tanh = sem("s_tanh")
        s_cT = sem("s_cT")
        s_cT_sb = sem("s_cT_sb")
        s_up = sem("s_up")
        s_hf = sem("s_hf")
        s_hhi = sem("s_hhi")
        s_hlo = sem("s_hlo")
        s_down = sem("s_down")
        s_prod = sem("s_prod")
        s_acc = sem("s_acc")
        s_fin = sem("s_fin")
        s_fin_sum = sem("s_fin_sum")
        s_fin_out = sem("s_fin_out")
        s_xT = sem("s_xT")
        s_xT_sb = sem("s_xT_sb")
        s_qk = sem("s_qk")
        s_qk_sb = sem("s_qk_sb")
        s_vk = sem("s_vk")
        s_v_sb = sem("s_v_sb")
        s_k0 = sem("s_k0")
        s_state = sem("s_state")
        s_state_sb = sem("s_state_sb")
        s_score = sem("s_score")
        s_A = sem("s_A")
        s_av = sem("s_av")
        s_gn = sem("s_gn")
        s_gn_ps = sem("s_gn_ps")
        s_gn_mean = sem("s_gn_mean")
        s_gn_ms = sem("s_gn_ms")
        s_gn_pow = sem("s_gn_pow")
        s_yn = sem("s_yn")
        s_wo = sem("s_wo")
        s_wo_sb = sem("s_wo_sb")
        s_zero = sem("s_zero")

        def slots_of(eng, slot, pairs_alone=0):
            slot(0, 0, first=True)
            with eng.Fori(0, NI // 2) as it:
                slot(it * 2 + 1, 1)
                slot(it * 2 + 2, 0)
            with eng.Fori(NI // 2, NI - 1 - pairs_alone) as it:
                slot(it * 2 + 1, 1, second=True)
                slot(it * 2 + 2, 0, second=True)
            for i in range(SLOTS - 1 - 2 * pairs_alone, SLOTS - 1):
                slot(i, i % 2, second=True)
            slot(SLOTS - 1, 1, second=True, last=True)

        block = ctx.enter_context(nc.Block())

        @block.sync
        def _(sp):
            x_pieces = x_rows.rearrange("(c t p) d -> c p t d", c=LNC, p=P)
            z_pieces = z_dram[0:B * T, :].rearrange("(c t p) d -> c p t d", c=LNC, p=P)
            sp.dma_start(xall[:, 0], x_pieces[0]).then_inc(s_xall[0], 16)
            sp.dma_start(cst[:], const).then_inc(s_const, 16)
            for n, w in enumerate((w_q, w_k, w_v, w_o)):
                sp.dma_start(wnat[:, n, :], w).then_inc(s_wnat, 16)
            for n in range(1, LNC):
                sp.dma_start(xall[:, n], x_pieces[n]).then_inc(s_xall[n], 16)
            for n in range(LNC):
                sp.wait_ge(s_ln, n + 1)
                sp.dma_start(z_pieces[n], xall[:, n]).then_inc(s_z_stored, 16)
            sp.wait_ge(s_z_stored, 16 * LNC)
            sp.dma_start(zt[:], item_rows(z_dram, 0)).then_inc(s_zt, 16)
            sp.dma_start(xt[:], batch_rows(z_dram, 0)).then_inc(s_xt, 16)
            sp.dma_start(xres[:], batch_rows(x_rows, 0)).then_inc(s_xres, 16)

            def load_item(j, i_done):
                wait(sp, s_zn, at(j, 1, 0))
                wait(sp, s_z_stored, (i_done + LNC) * 16)
                sp.dma_start(zt[:], item_rows(z_dram, j)).then_inc(s_zt, 16)

            def spread(j, par, prods):
                sp.wait_ge(s_cT_sb, at(j, 1, 1))
                rows = c_dram[bass.ds(j * (E * TI), E * TI), :]
                sp.dma_start(rows, combine_T[:]).then_inc(s_c_stored, 16)
                wait(sp, s_prod, prods)
                sp.wait_ge(s_c_stored, at(j, 16, 16))
                flat = rows.rearrange("(o r) p -> o (r p)", o=1).broadcast_to([P, E * ITEM])
                sp.dma_start(cbc[:, par].rearrange("p e t -> p (e t)"), flat).then_inc(s_cbc, 16)

            spread(0, 0, 0)
            load_item(1, 0)

            def finish_loads(i, second):
                sp.dma_start(base[:], item_rows(z_dram, i)).then_inc(s_base, 16)
                if second:
                    sp.wait_ge(s_xa_stored, (i - NI) * 32 + 32)
                    sp.dma_start(xa_in[:], item_rows(xa_dram, i - NI)).then_inc(s_xa_in, 16)

            def finish_store(i, second):
                if second:
                    sp.wait_ge(s_fin_out, at(i - NI, 1, 1))
                else:
                    sp.wait_ge(s_fin_sum, at(i, 1, 1))
                dst = item_rows(out_rows, i - NI) if second else item_rows(z_dram, i + NI)
                sp.dma_start(dst, res[:]).then_inc(s_z_stored, 16)

            def slot(i, par, first=False, second=False, last=False):
                if not first:
                    finish_loads(i - 1, second)
                if not last:
                    sp.wait_ge(s_xT, at(i, 1, 1))
                    sp.dma_start(xt[:], batch_rows(z_dram, i + 1)).then_inc(s_xt, 16)
                    if not (isinstance(i, int) and i == SLOTS - 2):
                        load_item(i + 2, 0 if first else i - 1)
                if not first:
                    finish_store(i - 1, second)
                if not last:
                    spread(i + 1, 1 - par, at(i, E, 0))
                sp.wait_ge(s_wo_sb, at(i, 1, 1))
                sp.dma_start(batch_rows(xa_dram, i), xa_out[:]).then_inc(s_xa_stored, 16)
                if not last:
                    sp.dma_start(xres[:], batch_rows(x_rows, i + 1)).then_inc(s_xres, 16)

            slots_of(sp, slot, pairs_alone=1)
            finish_loads(SLOTS - 1, True)
            finish_store(SLOTS - 1, True)
            sp.wait_ge(s_z_stored, 16 * (LNC + SLOTS))
            sp.wait_ge(s_xa_stored, 16 * B)
            sp.wait_ge(s_c_stored, 16 * SLOTS)

        @block.tensor
        def _(pe):
            pe.wait_ge(s_const, 16)
            pe.wait_ge(s_wnat, 64)
            for n in range(4):
                mm = pe.transpose(up[0][:, n * P:(n + 1) * P], wnat[:, n, :], ident)
            mm.then_inc(s_wtp, 1)
            pe.wait_ge(s_rnat, 32)
            pe.transpose(up[1][:, 0:NR], rnat[:, :], ident[0:NR, 0:NR]).then_inc(s_wtp, 1)
            for grp in range(2 * K // 4):
                if grp == 0:
                    pe.wait_ge(s_w1nat, 16)
                if grp == K // 4:
                    pe.wait_ge(s_w2nat, 16)
                pe.wait_ge(s_whi, grp + 1)
                if grp >= 1:
                    pe.wait_ge(s_wlo, grp)
                for n in range(4):
                    c = grp * 4 + n
                    src = w1nat[:, c, :] if c < K else w2nat_block(c - K)
                    mm = pe.transpose(up[grp % 2][:, n * P:(n + 1) * P], src, ident)
                mm.then_inc(s_wtp, 1)

            def prep_transpose(j, par):
                pe.wait_ge(s_zn, at(j, 1, 1))
                wait(pe, s_cT_sb, at(j, 1, 0))
                for t in range(TI):
                    mm = pe.transpose(pp[:, t * P:(t + 1) * P], zn[:, t, :], ident)
                mm.then_inc(s_zT, 1)

            def prep_logits(j, par):
                pe.wait_ge(s_zlo, at(j, 1, 1))
                for t in range(TI):
                    o = pp[:, t * NR:(t + 1) * NR]
                    hi, lo = zhi[:, par, t * P:(t + 1) * P], zlo[:, par, t * P:(t + 1) * P]
                    pe.matmul(o, hi, rhi[:], start=True, stop=False)
                    pe.matmul(o, hi, rlo[:], start=False, stop=False)
                    mm = pe.matmul(o, lo, rhi[:], start=False, stop=True)
                mm.then_inc(s_logit, 1)

            def prep_combine(j):
                pe.wait_ge(s_router, at(j, ROUTER_OPS, ROUTER_OPS))
                pe.transpose(pp[0:E * TI, 0:P], combine[:].rearrange("p g k t -> p (g k t)"), ident)\
                    .then_inc(s_cT, 1)

            def expert_up(i, par, k):
                if k == 0:
                    pe.wait_ge(s_zlo, at(i, 1, 1))
                wait(pe, s_hhi, at(i, K, k - 1))
                o = up[k % 2][:, :]
                pe.matmul(o, w1hi[:, k, :], zhi[:, par, :], start=True, stop=False)
                pe.matmul(o, w1lo[:, k, :], zhi[:, par, :], start=False, stop=False)
                pe.matmul(o, w1hi[:, k, :], zlo[:, par, :], start=False, stop=True).then_inc(s_up, 1)

            def expert_down(i, k):
                e, first = k // FC, k % FC == 0
                pe.wait_ge(s_hlo, at(i, K, k + 1))
                if first:
                    wait(pe, s_prod, at(i, E, e - 1))
                o = down[e % 2][:, :]
                pe.matmul(o, w2hi[:, k, :], hhi[:, k % RING, :], start=first, stop=False)
                pe.matmul(o, w2lo[:, k, :], hhi[:, k % RING, :], start=False, stop=False)
                pe.matmul(o, w2hi[:, k, :], hlo[:, k % RING, :], start=False, stop=not first)\
                    .then_inc(s_down, 1)

            def finish(i, par):
                pe.wait_ge(s_acc, at(i, E - 1, E - 1))
                pe.wait_ge(s_logit_sb, at(i, 1, 1) if isinstance(i, int) and i == SLOTS - 1 else at(i, 1, 2))
                for t in range(TI):
                    mm = pe.transpose(pp[:, t * P:(t + 1) * P], acc[:, par, t * P:(t + 1) * P], ident)
                mm.then_inc(s_fin, 1)

            def ret_transpose(i):
                pe.wait_ge(s_xt, at(i, 16, 16))
                wait(pe, s_gn_mean, at(i, 1, 0))
                for t in range(TB):
                    mm = pe.transpose(m0[:, t * P:(t + 1) * P], xt[:, t, :], ident)
                mm.then_inc(s_xT, 1)

            def ret_qk(i):
                pe.wait_ge(s_xT_sb, at(i, 1, 1))
                wait(pe, s_wo_sb, at(i, 1, 0))
                pe.matmul(m1[:, 0:T], wT[:, 0, :], xT[:], start=True, stop=True)
                pe.matmul(m1[:, T:2 * T], wT[:, 1, :], xT[:], start=True, stop=True).then_inc(s_qk, 1)

            def ret_vk(i):
                for t in range(TB):
                    mm = pe.matmul(m0[:, t * T:(t + 1) * T], xT[:, t * P:(t + 1) * P],
                                   wT[:, 1:3, :].rearrange("p a n -> p (a n)"), start=True, stop=True)
                mm.then_inc(s_vk, 1)

            def ret_state(i):
                pe.wait_ge(s_k0, at(i, 1, 1))
                pe.wait_ge(s_v_sb, at(i, V_COPIES, V_COPIES))
                pe.wait_ge(s_qk_sb, at(i, QK_OPS, QK_OPS))
                pe.matmul(m1[:, 0:P], k0[:], v0[:], start=True, stop=True).then_inc(s_state, 1)

            def ret_score(i, t, g):
                o = (m0, m1)[g % 2]
                if t == 0 and g == 1:
                    pe.wait_ge(s_state_sb, at(i, 1, 1))
                n = t * G + g
                if n >= 2:
                    pe.wait_ge(s_A, at(i, TB * G, n - 1))
                rows = slice(32 * g, 32 * g + 32)
                pe.matmul(o[:, :], kT[rows, t * P:(t + 1) * P], qblk[rows, :, t * P:(t + 1) * P],
                          start=True, stop=True, tile_position=(32 * g, 0)).then_inc(s_score, 1)

            def ret_av(i, t):
                pe.wait_ge(s_A, at(i, TB * G, (t + 1) * G))
                o = yy[:, t * P:(t + 1) * P]
                if t == 0:
                    wait(pe, s_yn, at(i, 1, 0))
                else:
                    pe.matmul(o, state[:], q1[:], start=True, stop=False, skip_group_check=True)
                for h in range(GH):
                    for g in range(G):
                        mm = pe.matmul(yy[32 * g:32 * g + 32, t * P:(t + 1) * P],
                                       vpad[:, t, g, h, :, :].rearrange("p a b -> p (a b)"),
                                       A[:, t, g, h, :], start=(t == 0 and h == 0), stop=(h == GH - 1),
                                       tile_position=(0, 32 * g), skip_group_check=True)
                mm.then_inc(s_av, 1)

            def ret_head_mean(i):
                pe.wait_ge(s_gn, at(i, GN_OPS, 6))
                pe.matmul(m0[:, 0:2], const_of("headmean"), ghm[:], start=True, stop=True)\
                    .then_inc(s_gn_ps, 1)

            def ret_out(i):
                pe.wait_ge(s_yn, at(i, 1, 1))
                for t in range(TB):
                    mm = pe.matmul(m1[:, t * P:(t + 1) * P], ynT[:, t * P:(t + 1) * P], wT[:, 3, :],
                                   start=True, stop=True)
                mm.then_inc(s_wo, 1)

            prep_transpose(0, 0)
            prep_logits(0, 0)
            prep_combine(0)

            def slot(i, par, first=False, second=False, last=False):
                for k in range(K):
                    expert_up(i, par, k)
                    if k >= LAG:
                        expert_down(i, k - LAG)
                    elif not first:
                        expert_down(i - 1, k - LAG + K)
                    if k == 0:
                        ret_transpose(i)
                    if k == 1:
                        ret_qk(i)
                    if k == 2:
                        ret_vk(i)
                    if k == 3:
                        if not last:
                            prep_transpose(i + 1, 1 - par)
                        ret_state(i)
                    if 4 <= k < 8:
                        n = 2 * (k - 4)
                        ret_score(i, n // G, n % G)
                        ret_score(i, (n + 1) // G, (n + 1) % G)
                    if k == 5 and not last:
                        prep_logits(i + 1, 1 - par)
                    if k == 7:
                        ret_av(i, 0)
                    if k == 8 and not first:
                        finish(i - 1, 1 - par)
                    if k == 9:
                        ret_av(i, 1)
                    if k == 12 and not last:
                        if not first:
                            pe.wait_ge(s_fin_sum, at(i, 1, 0))
                        prep_combine(i + 1)
                    if k == 12:
                        ret_head_mean(i)
                    if k == 15:
                        ret_out(i)

            slots_of(pe, slot)
            for k in range(K - LAG, K):
                expert_down(SLOTS - 1, k)
            finish(SLOTS - 1, 1)

        @block.scalar
        def _(act):
            act.dma_start(rnat[0:NG, :], w_macro).then_inc(s_rnat, 16)
            act.dma_start(rnat[NG:NR, :], w_micro.rearrange("g e d -> (g e) d")).then_inc(s_rnat, 16)
            act.dma_start(vecs[:, 0:1], norm_w.rearrange("(p o) -> p o", o=1)).then_inc(s_vecs, 16)
            act.dma_start(vecs[:, 1:2], gn_weight.rearrange("(p o) -> p o", o=1)).then_inc(s_vecs, 16)
            act.dma_start(vecs[:, 2:3], gn_bias.rearrange("(p o) -> p o", o=1)).then_inc(s_vecs, 16)
            act.dma_start(w1nat[:], w1.rearrange("e (c p) d -> p (e c) d", p=P)).then_inc(s_w1nat, 16)
            act.dma_start(w2nat, w2.rearrange("e d f -> d e f")).then_inc(s_w2nat, 16)
            act.wait_ge(s_wtp, 1)
            act.activation(wT[:].rearrange("p a n -> p (a n)"), up[0][:, :], ACT.Copy).then_inc(s_whi, 1)
            for grp in range(1 + 2 * K // 4):
                act.wait_ge(s_wtp, grp + 2)
                if grp == 0:
                    act.activation(rhi[:], up[1][:, 0:NR], ACT.Copy).then_inc(s_whi, 1)
                    continue
                c = (grp - 1) * 4
                dst = w1hi[:, c:c + 4, :] if c < K else w2hi[:, c - K:c - K + 4, :]
                act.activation(dst.rearrange("p a n -> p (a n)"), up[(grp - 1) % 2][:, :], ACT.Copy)\
                    .then_inc(s_whi, 1)
            act.wait_ge(s_vecs, 48)

            def prep_high(j, par):
                act.wait_ge(s_zT, at(j, 1, 1))
                wait(act, s_up, at(j, K, -K))
                act.activation(zhi[:, par, :], pp[:, :], ACT.Copy, scale=norm_col).then_inc(s_zhi, 1)

            def router_tanh(j):
                act.wait_ge(s_router, at(j, ROUTER_OPS, 5))
                act.activation(rt[:, 6, :], rt[:, 5, :], ACT.Tanh, scale=0.5).then_inc(s_tanh, 1)
                act.activation(rt[:, 7, :], rt[:, 3, :], ACT.Abs).then_inc(s_tanh, 1)
                act.wait_ge(s_tanh, at(j, 3, 2))
                act.activation(rt[:, 8, :], rt[:, 7, :], ACT.Tanh, scale=0.5).then_inc(s_tanh, 1)

            def prep_combine(j):
                act.wait_ge(s_cT, at(j, 1, 1))
                wait(act, s_c_stored, at(j, 16, 0))
                act.activation(combine_T[:], pp[0:E * TI, 0:P], ACT.Copy).then_inc(s_cT_sb, 1)

            def hidden(i, k):
                act.wait_ge(s_up, at(i, K, k + 1))
                wait(act, s_hlo, at(i, K, k + 1 - RING))
                act.activation(hf[:, k % RING, :], up[k % 2][:, :], ACT.Silu).then_inc(s_hf, 1)
                wait(act, s_down, at(i, K, k + 1 - RING))
                act.activation(hhi[:, k % RING, :], up[k % 2][:, :], ACT.Silu).then_inc(s_hhi, 1)

            def ret_xT(i):
                act.wait_ge(s_xT, at(i, 1, 1))
                wait(act, s_vk, at(i, 1, 0))
                act.activation(xT[:], m0[:, 0:T], ACT.Copy).then_inc(s_xT_sb, 1)

            def ret_v(i):
                act.wait_ge(s_vk, at(i, 1, 1))
                wait(act, s_av, at(i, TB, 0))
                for t in range(TB):
                    src = m0[:, t * T + P:(t + 1) * T].rearrange("p (g h d) -> p g h d", g=G, h=GH)
                    flat = vpad[:, t].rearrange("p g h a d -> p g (h a) d")[:, :, ::GH + 1, :]
                    act.activation(flat, src, ACT.Copy).then_inc(s_v_sb, 1)
                act.activation(v0[:], m0[:, P:T], ACT.Copy).then_inc(s_v_sb, 1)

            def ret_norm(i):
                act.wait_ge(s_gn, at(i, GN_OPS, GN_OPS))
                wait(act, s_wo, at(i, 1, 0))
                act.activation(ynT[:], yy[:, 0:T], ACT.Identity, scale=gv[:, 2:3], bias=gv[:, 3:4])\
                    .then_inc(s_yn, 1)

            act.wait_ge(s_zero, 1)
            prep_high(0, 0)
            router_tanh(0)
            prep_combine(0)

            def slot(i, par, first=False, second=False, last=False):
                for k in range(K):
                    hidden(i, k)
                    if k == 0:
                        ret_xT(i)
                    if k == 2:
                        ret_v(i)
                    if not last:
                        if k == 3:
                            prep_high(i + 1, 1 - par)
                        if k == 6:
                            router_tanh(i + 1)
                        if k == 12:
                            prep_combine(i + 1)
                    if k == 13:
                        ret_norm(i)

            slots_of(act, slot)

        @block.vector
        def _(dve):
            dve.memset(vpad[:].rearrange("p t g h a d -> p (t g h a d)"), 0.0).then_inc(s_zero, 1)

            s_chain = s_ln_chain
            done = [0]

            def link(ins):
                done[0] += 1
                ins.then_inc(s_chain, 1)
                return done[0]

            for c in range(LNC):
                dve.wait_ge(s_xall[c], 16)
                for t in range(LNT):
                    n = link(dve.bn_stats(stats[:, c, t, :], xall[:, c, t, :]))
                dve.wait_ge(s_chain, n)
                st = [stats[:, c, :, f] for f in range(6)]
                mean2, diff, m2, sq, var, mean = (ln[:, c, f, :] for f in range(6))
                link(dve.tensor_tensor(mean2, st[1], st[4], ALU.add))
                link(dve.tensor_tensor(diff, st[1], st[4], ALU.subtract))
                n = link(dve.tensor_tensor(m2, st[2], st[5], ALU.add))
                dve.wait_ge(s_chain, n)
                link(dve.tensor_scalar(mean, mean2, 0.5, None, ALU.mult))
                link(dve.tensor_tensor(sq, diff, diff, ALU.mult))
                n = link(dve.tensor_scalar(m2, m2, 1.0 / D, LN_EPS, ALU.mult, ALU.add))
                dve.wait_ge(s_chain, n)
                dve.scalar_tensor_tensor(out=var, in0=sq, scalar=0.25, in1=m2, op0=ALU.mult, op1=ALU.add)\
                    .then_inc(s_ln_var, 1)
                xc = xall[:, c]
                n = link(dve.tensor_tensor(xc, xc, mean.unsqueeze(2).broadcast_to([P, LNT, D]), ALU.subtract))
                dve.wait_ge(s_chain, n)
                dve.wait_ge(s_ln_pow, c + 1)
                dve.tensor_tensor(xc, xc, mean2.unsqueeze(2).broadcast_to([P, LNT, D]), ALU.mult)\
                    .then_inc(s_ln, 1)

            dve.wait_ge(s_whi, 2)
            dve.tensor_tensor(rlo[:], up[1][:, 0:NR], rhi[:].bitcast(F32), ALU.subtract).then_inc(s_wlo, 1)
            for grp in range(2 * K // 4):
                c = grp * 4
                hi, lo = (w1hi, w1lo) if c < K else (w2hi, w2lo)
                c %= K
                dve.wait_ge(s_whi, grp + 3)
                dve.tensor_tensor(lo[:, c:c + 4, :].rearrange("p a n -> p (a n)"), up[grp % 2][:, :],
                                  hi[:, c:c + 4, :].bitcast(F32).rearrange("p a n -> p (a n)"),
                                  ALU.subtract).then_inc(s_wlo, 1)
            dve.wait_ge(s_vecs, 48)

            def prep_mean_square(j):
                dve.wait_ge(s_sq, at(j, 1, 1))
                dve.tensor_reduce(ms[:, 0, :], zn[:], AX_X, ALU.add).then_inc(s_ms, 1)
                dve.wait_ge(s_ms, at(j, 2, 1))
                dve.tensor_scalar(ms[:, 1, :], ms[:, 0, :], 1.0 / D, RMS_EPS, ALU.mult, ALU.add)\
                    .then_inc(s_ms, 1)

            def prep_low(j, par):
                dve.wait_ge(s_zhi, at(j, 1, 1))
                dve.scalar_tensor_tensor(out=zlo[:, par, :], in0=pp[:, :], scalar=norm_col,
                                         in1=zhi[:, par, :].bitcast(F32), op0=ALU.mult, op1=ALU.subtract)\
                    .then_inc(s_zlo, 1)

            def prep_logits(j):
                dve.wait_ge(s_logit, at(j, 1, 1))
                dve.tensor_copy(logit[:].rearrange("p t c -> p (t c)"), pp[:, 0:TI * NR]).then_inc(s_logit_sb, 1)

            def row(n):
                return rt[:, n, :].rearrange("p (t g) -> p t g", t=TI)

            def one(n):
                return rt[:, n, 0:TI]

            def wide(ap):
                return ap.unsqueeze(2).broadcast_to([P, TI, NG])

            def router(j, part):
                m = logit[:, :, 0:NG]
                u = logit[:, :, NG:NR].rearrange("p t (g k) -> p t g k", k=PG)

                def need(n):
                    dve.wait_ge(s_router, at(j, ROUTER_OPS, n))

                if part == 0:
                    dve.wait_ge(s_logit_sb, at(j, 1, 1))
                    dve.tensor_reduce(one(0), m, AX_X, ALU.max).then_inc(s_router, 1)
                    dve.tensor_tensor(beats[:, 0], m.unsqueeze(3).broadcast_to([P, TI, NG, NG]),
                                      m.unsqueeze(2).broadcast_to([P, TI, NG, NG]), ALU.is_gt)\
                        .then_inc(s_router, 1)
                    dve.tensor_tensor(row(3), u[:, :, :, 0], u[:, :, :, 1], ALU.subtract)\
                        .then_inc(s_router, 1)
                    dve.tensor_tensor(row(4), u[:, :, :, 0], u[:, :, :, 1], ALU.is_ge)\
                        .then_inc(s_router, 1)
                    need(1)
                    dve.tensor_tensor(row(5), m, wide(one(0)), ALU.subtract).then_inc(s_router, 1)
                    need(2)
                    early = const_of("earlier").rearrange("p (o i j) -> p o i j", o=1, i=NG)\
                        .broadcast_to([P, TI, NG, NG])
                    dve.tensor_tensor(beats[:, 1], beats[:, 0], early, ALU.mult).then_inc(s_router, 1)
                if part == 1:
                    need(6)
                    dve.tensor_tensor(beats[:, 2], beats[:, 1], beats[:, 1].rearrange("p t i j -> p t j i"),
                                      ALU.subtract).then_inc(s_router, 1)
                    need(7)
                    dve.tensor_reduce(row(9), beats[:, 2], AX_X, ALU.add).then_inc(s_router, 1)
                    need(8)
                    dve.tensor_tensor(row(10), row(9),
                                      const_of("wins_needed").unsqueeze(1).broadcast_to([P, TI, NG]),
                                      ALU.is_ge).then_inc(s_router, 1)
                if part == 2:
                    dve.wait_ge(s_tanh, at(j, 3, 3))
                    dve.tensor_scalar(row(11), row(6), -1.0, 1.0, ALU.mult, ALU.add)\
                        .then_inc(s_router, 1)
                    dve.tensor_scalar(row(12), row(8), 0.5, 0.5, ALU.mult, ALU.add)\
                        .then_inc(s_router, 1)
                    need(10)
                    dve.reciprocal(row(13), row(11)).then_inc(s_router, 1)
                    need(11)
                    dve.tensor_scalar(row(14), row(12), TOPK_EPS, None, ALU.add)\
                        .then_inc(s_router, 1)
                    need(12)
                    dve.scalar_tensor_tensor(out=rt[:, 15, :], in0=rt[:, 6, :], scalar=1.0,
                                             in1=rt[:, 13, :], op0=ALU.add, op1=ALU.mult)\
                        .then_inc(s_router, 1)
                if part == 3:
                    need(14)
                    dve.tensor_tensor(row(16), row(15), row(10), ALU.mult).then_inc(s_router, 1)
                    dve.tensor_reduce(one(17), row(15), AX_X, ALU.add).then_inc(s_router, 1)
                    need(15)
                    dve.tensor_reduce(one(18), row(16), AX_X, ALU.add).then_inc(s_router, 1)
                    dve.tensor_tensor(row(21), row(16), row(12), ALU.mult).then_inc(s_router, 1)
                    need(17)
                    dve.scalar_tensor_tensor(out=one(19), in0=one(17), scalar=TOPK_EPS, in1=one(18),
                                             op0=ALU.mult, op1=ALU.add).then_inc(s_router, 1)
                if part == 4:
                    need(19)
                    dve.tensor_tensor(row(20), row(14), wide(one(19)), ALU.mult).then_inc(s_router, 1)
                    need(20)
                    dve.reciprocal(row(22), row(20)).then_inc(s_router, 1)
                    need(21)
                    dve.tensor_tensor(row(23), row(21), row(22), ALU.mult).then_inc(s_router, 1)
                    need(22)
                    wait(dve, s_cT, at(j, 1, 0))
                    picked = combine[:].rearrange("p g k t -> p k t g")
                    dve.tensor_tensor(picked[:, 0], row(23), row(4), ALU.mult).then_inc(s_router, 1)
                    need(23)
                    dve.tensor_tensor(picked[:, 1], row(23), picked[:, 0], ALU.subtract)\
                        .then_inc(s_router, 1)

            def low(i, k):
                dve.wait_ge(s_hhi, at(i, K, k + 1))
                wait(dve, s_down, at(i, K, k + 1 - RING))
                dve.tensor_tensor(hlo[:, k % RING, :], hf[:, k % RING, :],
                                  hhi[:, k % RING, :].bitcast(F32), ALU.subtract).then_inc(s_hlo, 1)

            def weigh(i, par, e):
                dve.wait_ge(s_down, at(i, K, FC * (e + 1)))
                if e == 0:
                    dve.wait_ge(s_cbc, at(i, 16, 16))
                    dst = acc[:, par, :]
                else:
                    wait(dve, s_acc, at(i, E - 1, e - 2) if e >= 2 else at(i, E - 1, 0))
                    dst = prod[:, e % 2, :]
                dve.tensor_tensor(dst, down[e % 2][:, :], cbc[:, par, e, :], ALU.mult).then_inc(s_prod, 1)

            def finish(i, second):
                dve.wait_ge(s_fin, at(i, 1, 1))
                dve.wait_ge(s_base, at(i, 16, 16))
                dve.wait_ge(s_z_stored, (i + LNC) * 16)
                flat = res[:].rearrange("p t d -> p (t d)")
                dve.tensor_tensor(flat, pp[:, :], base[:].rearrange("p t d -> p (t d)"), ALU.add)\
                    .then_inc(s_fin_sum, 1)
                if second:
                    dve.wait_ge(s_fin_sum, at(i, 1, 1))
                    dve.wait_ge(s_xa_in, at(i - NI, 16, 16))
                    dve.tensor_tensor(flat, flat, xa_in[:].rearrange("p t d -> p (t d)"), ALU.add)\
                        .then_inc(s_fin_out, 1)

            def ret_qk(i):
                dve.wait_ge(s_qk, at(i, 1, 1))
                wait(dve, s_av, at(i, TB, 0))
                dve.tensor_tensor(qblk[:], m1[:, 0:T].unsqueeze(1).broadcast_to([P, GH, T]),
                                  const_of("qdecay").rearrange("p (h t) -> p h t", h=GH), ALU.mult)\
                    .then_inc(s_qk_sb, 1)
                dve.tensor_tensor(q1[:], m1[:, P:T], const_of("qdecay_plain"), ALU.mult).then_inc(s_qk_sb, 1)
                dve.tensor_tensor(kT[:], m1[:, T:2 * T], const_of("kdecay"), ALU.mult).then_inc(s_qk_sb, 1)

            def ret_k0(i):
                dve.wait_ge(s_v_sb, at(i, V_COPIES, V_COPIES))
                dve.tensor_tensor(k0[:], m0[:, 0:P], const_of("kdecay_tok"), ALU.mult).then_inc(s_k0, 1)

            def ret_state(i):
                dve.wait_ge(s_state, at(i, 1, 1))
                dve.tensor_tensor(state[:], m1[:, 0:P], const_of("headmask"), ALU.mult)\
                    .then_inc(s_state_sb, 1)

            def ret_mask(i, n):
                dve.wait_ge(s_score, at(i, TB * G, n + 1))
                t, g = n // G, n % G
                src = (m0, m1)[g % 2][:, :].rearrange("p (h q) -> p h q", h=GH)
                dve.tensor_tensor(A[:, t, g], src, const_of("causal").unsqueeze(1).broadcast_to([P, GH, P]),
                                  ALU.mult).then_inc(s_A, 1)

            def ret_stats(i):
                dve.wait_ge(s_av, at(i, TB, TB))
                dve.bn_stats(gst[:], yy[:, 0:T]).then_inc(s_gn, 1)
                dve.wait_ge(s_gn, at(i, GN_OPS, 1))
                me, ve, mo, vo = gst[:, 1:2], gst[:, 2:3], gst[:, 4:5], gst[:, 5:6]
                dve.tensor_scalar(ghm[:, 0:1], me, mo, 0.5, ALU.add, ALU.mult).then_inc(s_gn, 1)
                dve.tensor_tensor(gsq[:, 0:1], me, me, ALU.mult).then_inc(s_gn, 1)
                dve.tensor_scalar(gsq[:, 1:2], ve, vo, 1.0 / T, ALU.add, ALU.mult).then_inc(s_gn, 1)
                dve.wait_ge(s_gn, at(i, GN_OPS, 3))
                dve.scalar_tensor_tensor(out=gsq[:, 2:3], in0=mo, scalar=mo, in1=gsq[:, 0:1],
                                         op0=ALU.mult, op1=ALU.add).then_inc(s_gn, 1)
                dve.wait_ge(s_gn, at(i, GN_OPS, 5))
                dve.scalar_tensor_tensor(out=ghm[:, 1:2], in0=gsq[:, 2:3], scalar=0.5, in1=gsq[:, 1:2],
                                         op0=ALU.mult, op1=ALU.add).then_inc(s_gn, 1)

            def ret_var(i):
                dve.wait_ge(s_gn_ps, at(i, 1, 1))
                dve.tensor_copy(gmv[:], m0[:, 0:2]).then_inc(s_gn_mean, 1)
                dve.wait_ge(s_gn_mean, at(i, 1, 1))
                dve.tensor_tensor(gv[:, 0:1], gmv[:, 0:1], gmv[:, 0:1], ALU.mult).then_inc(s_gn, 1)
                dve.wait_ge(s_gn, at(i, GN_OPS, 7))
                dve.scalar_tensor_tensor(out=gv[:, 1:2], in0=gmv[:, 1:2], scalar=LN_EPS, in1=gv[:, 0:1],
                                         op0=ALU.add, op1=ALU.subtract).then_inc(s_gn, 1)

            def ret_affine(i):
                dve.wait_ge(s_gn_pow, at(i, 1, 1))
                dve.tensor_tensor(gv[:, 2:3], gst[:, 0:1], gnw_col, ALU.mult).then_inc(s_gn, 1)
                dve.wait_ge(s_gn, at(i, GN_OPS, 9))
                dve.tensor_tensor(gst[:, 1:2], gmv[:, 0:1], gv[:, 2:3], ALU.mult).then_inc(s_gn_ms, 1)
                dve.wait_ge(s_gn_ms, at(i, 1, 1))
                dve.tensor_tensor(gv[:, 3:4], gnb_col, gst[:, 1:2], ALU.subtract).then_inc(s_gn, 1)

            def ret_residual(i):
                dve.wait_ge(s_wo, at(i, 1, 1))
                dve.wait_ge(s_xres, at(i, 16, 16))
                wait(dve, s_xa_stored, at(i, 16, 0))
                dve.tensor_tensor(xa_out[:].rearrange("p t d -> p (t d)"), m1[:, 0:T],
                                  xres[:].rearrange("p t d -> p (t d)"), ALU.add).then_inc(s_wo_sb, 1)

            prep_mean_square(0)
            prep_low(0, 0)
            prep_logits(0)
            for part in range(5):
                router(0, part)

            def slot(i, par, first=False, second=False, last=False):
                for k in range(K):
                    low(i, k)
                    if k % 2 == 0:
                        if k >= 4:
                            weigh(i, par, (k - 4) // 2)
                        elif not first:
                            weigh(i - 1, 1 - par, E - 2 + k // 2)
                    if k == 0 and not last:
                        prep_mean_square(i + 1)
                    if k == 1:
                        ret_qk(i)
                    if k == 2:
                        ret_k0(i)
                    if k == 3:
                        if not last:
                            prep_low(i + 1, 1 - par)
                        ret_state(i)
                    if 4 <= k < 8:
                        ret_mask(i, 2 * (k - 4))
                        ret_mask(i, 2 * (k - 4) + 1)
                    if not last:
                        if k == 5:
                            prep_logits(i + 1)
                        if 6 <= k < 11:
                            router(i + 1, k - 6)
                    if k == 8 and not first:
                        finish(i - 1, second)
                    if k == 10:
                        ret_stats(i)
                    if k == 12:
                        ret_var(i)
                    if k == 13:
                        ret_affine(i)
                    if k == 15:
                        ret_residual(i)

            slots_of(dve, slot)
            weigh(SLOTS - 1, 1, E - 2)
            weigh(SLOTS - 1, 1, E - 1)
            finish(SLOTS - 1, True)

        @block.gpsimd
        def _(pool):
            half = const_of("minus_half")
            pool.wait_ge(s_const, 16)
            for c in range(LNC):
                pool.wait_ge(s_ln_var, c + 1)
                pool.tensor_tensor(ln[:, c, 0, :], ln[:, c, 4, :], half[:, 0:LNT], ALU.pow)\
                    .then_inc(s_ln_pow, 1)

            def prep_square(j):
                pool.wait_ge(s_zt, at(j, 16, 16))
                wait(pool, s_zT, at(j, 1, 0))
                pool.tensor_tensor(zn[:], zt[:], zt[:], ALU.mult).then_inc(s_sq, 1)

            def prep_norm(j):
                pool.wait_ge(s_ms, at(j, 2, 2))
                pool.tensor_tensor(rstd[:], ms[:, 1, :], half[:, 0:TI], ALU.pow).then_inc(s_rstd, 1)
                pool.wait_ge(s_rstd, at(j, 1, 1))
                pool.tensor_tensor(zn[:], zt[:], rstd[:].unsqueeze(2).broadcast_to([P, TI, D]), ALU.mult)\
                    .then_inc(s_zn, 1)

            def add(i, par, e):
                pool.wait_ge(s_prod, at(i, E, e + 1))
                if e > 1:
                    pool.wait_ge(s_acc, at(i, E - 1, e - 1))
                pool.tensor_tensor(acc[:, par, :], acc[:, par, :], prod[:, e % 2, :], ALU.add)\
                    .then_inc(s_acc, 1)

            prep_square(0)
            prep_norm(0)

            def slot(i, par, first=False, second=False, last=False):
                if not last:
                    prep_square(i + 1)
                if not first:
                    add(i - 1, 1 - par, E - 2)
                if not last:
                    prep_norm(i + 1)
                if not first:
                    add(i - 1, 1 - par, E - 1)
                for e in range(1, E - 2):
                    if e == E - 3:
                        pool.wait_ge(s_gn, at(i, GN_OPS, 8))
                        pool.tensor_tensor(gst[:, 0:1], gv[:, 1:2], half[:, 0:1], ALU.pow)\
                            .then_inc(s_gn_pow, 1)
                    add(i, par, e)

            slots_of(pool, slot)
            add(SLOTS - 1, 1, E - 2)
            add(SLOTS - 1, 1, E - 1)


_INS = ["L0_attn_x", "L0_attn_W_q", "L0_attn_W_k", "L0_attn_W_v", "L0_attn_W_o", "L0_attn_gn_weight",
        "L0_attn_gn_bias", "L0_ffn_norm_w", "L0_ffn_w_macro", "L0_ffn_w_micro", "L0_ffn_w1", "L0_ffn_w2"]


def kernel(**inputs):
    import numpy as _np
    import concourse.bacc as _bacc
    from concourse import mybir as _mybir
    from concourse.bass_utils import run_bass_kernel_spmd as _run

    nc = _bacc.Bacc("TRN2", target_bir_lowering=False, num_devices=1)
    arrays, args = {}, []
    for name in _INS:
        a = _np.ascontiguousarray(inputs[name])
        arrays[f"in_{name}_dram"] = a
        args.append(nc.dram_tensor(f"in_{name}_dram", a.shape, _mybir.dt.from_np(a.dtype), kind="ExternalInput").ap())
    arrays["constants_dram"] = constants()
    args.append(nc.dram_tensor("constants_dram", (P, NCONST), F32, kind="ExternalInput").ap())
    args.append(nc.dram_tensor("out_0_dram", (B, T, D), F32, kind="ExternalOutput").ap())
    program(nc, *args)
    r = _run(nc, [arrays], core_ids=[0])
    return r.results[0]["out_0_dram"]
```

```python
from contextlib import ExitStack

import concourse.bass as bass
from concourse import mybir

F32 = mybir.dt.float32
F32R = mybir.dt.float32r
ALU = mybir.AluOpType
ACT = mybir.ActivationFunctionType
AX_X = mybir.AxisListType.X

P = 128
B, T, D = 16, 256, 128
H = 16
DH = D // H
GH = 4
G = H // GH
TB = T // P
ITEM = 512
TI = ITEM // P
NI = B * T // ITEM
SLOTS = 2 * NI
E = 8
NG, PG = 4, 2
F = 256
FC = F // P
K = E * FC
LAG = 3
RING = 4
NR = NG + E
LN_EPS = 1e-5
RMS_EPS = 1e-6
TOPK_EPS = 1e-9
LNC = NI
LNT = B * T // P // LNC

CONST = {}
_at = 0
for _name, _w in (("ident", P), ("earlier", NG * NG), ("wins_needed", NG), ("minus_half", 8),
                  ("qdecay", GH * T), ("kdecay", T), ("kdecay_tok", P), ("qdecay_plain", P),
                  ("headmask", P), ("causal", P), ("headmean", P)):
    CONST[_name] = (_at, _at + _w)
    _at += _w
NCONST = _at
NFIRST = CONST["qdecay"][0]

WGROUPS = 2 + 2 * K // 4
LN_BEFORE = 3
ROUTER_OPS = 24
V_COPIES = 3
QK_OPS = 3
GN_OPS = 10


def constants():
    import numpy as np

    c = np.zeros((P, NCONST), np.float32)

    def put(name, a):
        lo, hi = CONST[name]
        c[:, lo:hi] = np.asarray(a, np.float64).reshape(a.shape[0], -1)

    head = np.arange(P) // DH
    gamma = 1.0 - 2.0 ** (-5.0 - np.arange(H))
    g = gamma[head][:, None]
    t = np.arange(T)[None, :]
    put("ident", np.eye(P))
    put("causal", np.triu(np.ones((P, P))))
    same = (head[:, None] == head[None, :]).astype(float)
    put("headmask", same)
    put("headmean", same / DH)
    put("kdecay_tok", (g ** -np.arange(P)[None, :]).T)
    put("kdecay", g ** -t)
    q = g ** t / np.sqrt(DH)
    mask = ((head % GH)[:, None, None] == np.arange(GH)[None, :, None]).astype(float)
    put("qdecay", mask * q[:, None, :])
    put("qdecay_plain", q[:, P:T])
    put("earlier", np.tile((np.arange(NG)[:, None] > np.arange(NG)[None, :]).astype(float)[None], (P, 1, 1)))
    put("wins_needed", np.tile(np.arange(NG)[None] - 1.0, (P, 1)))
    put("minus_half", np.full((P, 8), -0.5))
    return c


def at(i, per_slot, nth):
    return i * per_slot + nth


def wait(eng, sem, value):
    if isinstance(value, int) and value <= 0:
        return
    eng.wait_ge(sem, value)


def program(nc, x, w_q, w_k, w_v, w_o, gn_weight, gn_bias, norm_w, w_macro, w_micro, w1, w2, const, out):
    z_dram = nc.dram_tensor("z_rounds", (2 * NI * ITEM, D), F32, kind="Internal").ap()
    xa_dram = nc.dram_tensor("x_plus_attn", (B * T, D), F32, kind="Internal").ap()
    c_dram = nc.dram_tensor("combine", (SLOTS * E * TI, P), F32, kind="Internal").ap()
    x_rows = x.rearrange("b t d -> (b t) d")
    out_rows = out.rearrange("b t d -> (b t) d")

    def item_rows(rows, i):
        return rows[bass.ds(i * ITEM, ITEM), :].rearrange("(t p) d -> p t d", p=P)

    def batch_rows(rows, b):
        return rows[bass.ds(b * T, T), :].rearrange("(t p) d -> p t d", p=P)

    with ExitStack() as ctx:
        def sb(name, shape, dt=F32):
            return ctx.enter_context(nc.sbuf_tensor(name, shape, dt))

        def bank(name):
            return ctx.enter_context(nc.psum_tensor(name, [P, 512], F32))

        def sem(name):
            return ctx.enter_context(nc.semaphore(name))

        cst = sb("cst", [P, NCONST])

        def const_of(name):
            return cst[:, CONST[name][0]:CONST[name][1]]

        ident = const_of("ident")
        vecs = sb("vecs", [P, 3])
        norm_col, gnw_col, gnb_col = (vecs[:, n:n + 1] for n in range(3))
        wnat = sb("wnat", [P, 4, D])
        rnat = sb("rnat", [NR, D])
        wT = sb("wT", [P, 4, D])
        rhi = sb("rhi", [P, P], F32R)
        rlo = sb("rlo", [P, P], F32R)
        w1hi = sb("w1hi", [P, K, P], F32R)
        w1lo = sb("w1lo", [P, K, P], F32R)
        w2hi = sb("w2hi", [P, K, P], F32R)
        w2lo = sb("w2lo", [P, K, P], F32R)
        xall = sb("xall", [P, LNC, LNT, D])
        w1nat = sb("w1nat", [P, K, D])
        w2nat_sb = sb("w2nat", [P, E, F])
        w2nat = w2nat_sb[:]

        def w2nat_block(c):
            return w2nat_sb[:, c // FC, (c % FC) * P:(c % FC + 1) * P]

        stats = sb("stats", [P, LNC, LNT, 6])
        ln = sb("ln", [P, LNC, 6, LNT])
        zt = sb("zt", [P, TI, D])
        zn = sb("zn", [P, TI, D])
        ms = sb("ms", [P, 2, TI])
        rstd = sb("rstd", [P, TI])
        zhi = sb("zhi", [P, 2, ITEM], F32R)
        zlo = sb("zlo", [P, 2, ITEM], F32R)
        lgT = sb("lgT", [P, ITEM])
        logit = sb("logit", [P, TI, NR])
        rt = sb("rt", [P, 24, TI * NG])
        beats = sb("beats", [P, 3, TI, NG, NG])
        combine = sb("combine_tok", [P, NG, PG, TI])
        combine_T = sb("combine_T", [E * TI, P])
        cbc = sb("cbc", [P, 2, E, ITEM])
        hf = sb("hf", [P, RING, ITEM])
        hhi = sb("hhi", [P, RING, ITEM], F32R)
        hlo = sb("hlo", [P, RING, ITEM], F32R)
        prod = sb("prod", [P, 2, ITEM])
        acc = sb("acc", [P, 2, ITEM])
        base = sb("base", [P, TI, D])
        xa_in = sb("xa_in", [P, TI, D])
        res = sb("res", [P, TI, D])
        xt = sb("xt", [P, TB, D])
        xres = sb("xres", [P, TB, D])
        xT = sb("xT", [P, T])
        qblk = sb("qblk", [P, GH, T])
        q1 = sb("q1", [P, P])
        kT = sb("kT", [P, T])
        vpad = sb("vpad", [P, TB, G, GH, GH, DH])
        v0 = sb("v0", [P, P])
        k0 = sb("k0", [P, P])
        state = sb("state", [P, P])
        A = sb("A", [P, TB, G, GH, P])
        gst = sb("gst", [P, 6])
        gsq = sb("gsq", [P, 3])
        gmv = sb("gmv", [P, 2])
        ghm = sb("ghm", [P, 2])
        gv = sb("gv", [P, 4])
        ynT = sb("ynT", [P, T])
        xa_out = sb("xa_out", [P, TB, D])

        up = [bank(f"up{n}") for n in range(2)]
        down = [bank(f"down{n}") for n in range(2)]
        m0, m1, pp, yy = bank("m0"), bank("m1"), bank("pp"), bank("yy")
        wbank = up + down

        s_const0 = sem("s_const0")
        s_const = sem("s_const")
        s_vecs = sem("s_vecs")
        s_wnat = sem("s_wnat")
        s_rnat = sem("s_rnat")
        s_w1nat = sem("s_w1nat")
        s_w2nat = sem("s_w2nat")
        s_xall = [sem(f"s_xall{n}") for n in range(LNC)]
        s_zt = sem("s_zt")
        s_xt = sem("s_xt")
        s_xres = sem("s_xres")
        s_base = sem("s_base")
        s_xa_in = sem("s_xa_in")
        s_cbc = sem("s_cbc")
        s_z_stored = sem("s_z_stored")
        s_xa_stored = sem("s_xa_stored")
        s_c_stored = sem("s_c_stored")
        s_wtp = sem("s_wtp")
        s_whi = sem("s_whi")
        s_wlo = sem("s_wlo")
        s_ln = sem("s_ln")
        s_ln_step = sem("s_ln_step")
        s_ln_var = sem("s_ln_var")
        s_ln_pow = sem("s_ln_pow")
        s_sq = sem("s_sq")
        s_ms = sem("s_ms")
        s_rstd = sem("s_rstd")
        s_zn = sem("s_zn")
        s_zT = sem("s_zT")
        s_zhi = sem("s_zhi")
        s_zlo = sem("s_zlo")
        s_lgT = sem("s_lgT")
        s_lgT_sb = sem("s_lgT_sb")
        s_logit = sem("s_logit")
        s_logit_sb = sem("s_logit_sb")
        s_router = sem("s_router")
        s_tanh = sem("s_tanh")
        s_cT = sem("s_cT")
        s_cT_sb = sem("s_cT_sb")
        s_up = sem("s_up")
        s_hf = sem("s_hf")
        s_hhi = sem("s_hhi")
        s_hlo = sem("s_hlo")
        s_down = sem("s_down")
        s_prod = sem("s_prod")
        s_acc = sem("s_acc")
        s_fin = sem("s_fin")
        s_fin_sum = sem("s_fin_sum")
        s_fin_out = sem("s_fin_out")
        s_xT = sem("s_xT")
        s_xT_sb = sem("s_xT_sb")
        s_qk = sem("s_qk")
        s_qk_sb = sem("s_qk_sb")
        s_vk = sem("s_vk")
        s_v_sb = sem("s_v_sb")
        s_k0 = sem("s_k0")
        s_state = sem("s_state")
        s_state_sb = sem("s_state_sb")
        s_score = sem("s_score")
        s_A = sem("s_A")
        s_av = sem("s_av")
        s_gn = sem("s_gn")
        s_gn_ps = sem("s_gn_ps")
        s_gn_mean = sem("s_gn_mean")
        s_gn_ms = sem("s_gn_ms")
        s_gn_pow = sem("s_gn_pow")
        s_yn = sem("s_yn")
        s_wo = sem("s_wo")
        s_wo_sb = sem("s_wo_sb")
        s_zero = sem("s_zero")

        def slots_of(eng, slot, pairs_alone=0):
            slot(0, 0, first=True)
            with eng.Fori(0, NI // 2) as it:
                slot(it * 2 + 1, 1)
                slot(it * 2 + 2, 0)
            with eng.Fori(NI // 2, NI - 1 - pairs_alone) as it:
                slot(it * 2 + 1, 1, second=True)
                slot(it * 2 + 2, 0, second=True)
            for i in range(SLOTS - 1 - 2 * pairs_alone, SLOTS - 1):
                slot(i, i % 2, second=True)
            slot(SLOTS - 1, 1, second=True, last=True)

        block = ctx.enter_context(nc.Block())

        @block.sync
        def _(sp):
            x_pieces = x_rows.rearrange("(c t p) d -> c p t d", c=LNC, p=P)
            z_pieces = z_dram[0:B * T, :].rearrange("(c t p) d -> c p t d", c=LNC, p=P)
            sp.dma_start(xall[:, 0], x_pieces[0]).then_inc(s_xall[0], 16)
            sp.dma_start(cst[:, 0:NFIRST], const[:, 0:NFIRST]).then_inc(s_const0, 16)
            for n, w in enumerate((w_q, w_k, w_v, w_o)):
                sp.dma_start(wnat[:, n, :], w).then_inc(s_wnat, 16)
            sp.dma_start(xall[:, 1], x_pieces[1]).then_inc(s_xall[1], 16)
            sp.dma_start(cst[:, NFIRST:], const[:, NFIRST:]).then_inc(s_const, 16)
            for n in range(2, LNC):
                sp.dma_start(xall[:, n], x_pieces[n]).then_inc(s_xall[n], 16)
            sp.dma_start(xres[:], batch_rows(x_rows, 0)).then_inc(s_xres, 16)

            def store_piece(n):
                sp.wait_ge(s_ln, n + 1)
                sp.dma_start(z_pieces[n], xall[:, n]).then_inc(s_z_stored, 16)

            store_piece(0)

            def load_item(j, stored):
                sp.wait_ge(s_zn, at(j, 1, 0))
                sp.wait_ge(s_z_stored, stored * 16)
                sp.dma_start(zt[:], item_rows(z_dram, j)).then_inc(s_zt, 16)

            def spread(j, par, prods):
                sp.wait_ge(s_cT_sb, at(j, 1, 1))
                rows = c_dram[bass.ds(j * (E * TI), E * TI), :]
                sp.dma_start(rows, combine_T[:]).then_inc(s_c_stored, 16)
                wait(sp, s_prod, prods)
                sp.wait_ge(s_c_stored, at(j, 16, 16))
                flat = rows.rearrange("(o r) p -> o (r p)", o=1).broadcast_to([P, E * ITEM])
                sp.dma_start(cbc[:, par].rearrange("p e t -> p (e t)"), flat).then_inc(s_cbc, 16)

            spread(0, 0, 0)
            for n in range(1, LN_BEFORE):
                store_piece(n)

            def finish_loads(i, second):
                sp.dma_start(base[:], item_rows(z_dram, i)).then_inc(s_base, 16)
                if second:
                    sp.wait_ge(s_xa_stored, (i - NI) * 32 + 32)
                    sp.dma_start(xa_in[:], item_rows(xa_dram, i - NI)).then_inc(s_xa_in, 16)

            def finish_store(i, second):
                if second:
                    sp.wait_ge(s_fin_out, at(i - NI, 1, 1))
                else:
                    sp.wait_ge(s_fin_sum, at(i, 1, 1))
                dst = item_rows(out_rows, i - NI) if second else item_rows(z_dram, i + NI)
                sp.dma_start(dst, res[:]).then_inc(s_z_stored, 16)

            def store_retention(b):
                sp.wait_ge(s_wo_sb, at(b, 1, 1))
                sp.dma_start(batch_rows(xa_dram, b), xa_out[:]).then_inc(s_xa_stored, 16)

            def slot(i, par, first=False, second=False, last=False):
                if not first:
                    finish_loads(i - 1, second)
                if not last:
                    sp.wait_ge(s_xT, at(i, 1, 1))
                    if first:
                        sp.wait_ge(s_z_stored, 16)
                    sp.dma_start(xt[:], batch_rows(z_dram, i + 1)).then_inc(s_xt, 16)
                if not first:
                    store_retention(i - 1)
                    sp.dma_start(xres[:], batch_rows(x_rows, i)).then_inc(s_xres, 16)
                if not last and not (isinstance(i, int) and i == SLOTS - 2):
                    load_item(i + 2, LN_BEFORE if first else LNC + i - 1)
                if first:
                    for n in range(LN_BEFORE, LNC):
                        store_piece(n)
                else:
                    finish_store(i - 1, second)
                if not last:
                    spread(i + 1, 1 - par, at(i, E, 0))

            slots_of(sp, slot, pairs_alone=1)
            store_retention(B - 1)
            finish_loads(SLOTS - 1, True)
            finish_store(SLOTS - 1, True)
            sp.wait_ge(s_z_stored, 16 * (LNC + SLOTS))
            sp.wait_ge(s_xa_stored, 16 * B)
            sp.wait_ge(s_c_stored, 16 * SLOTS)

        @block.tensor
        def _(pe):
            pe.wait_ge(s_const0, 16)

            def weights(n):
                o = wbank[n % 4]
                if n >= 4:
                    pe.wait_ge(s_whi, n - 3)
                    wait(pe, s_wlo, n - 4)
                if n == 0:
                    pe.wait_ge(s_wnat, 64)
                    for m in range(4):
                        mm = pe.transpose(o[:, m * P:(m + 1) * P], wnat[:, m, :], ident)
                elif n == 1:
                    pe.wait_ge(s_rnat, 32)
                    mm = pe.transpose(o[:, 0:NR], rnat[:, :], ident[0:NR, 0:NR])
                else:
                    pe.wait_ge(s_w1nat if n < 2 + K // 4 else s_w2nat, 16)
                    for m in range(4):
                        c = (n - 2) * 4 + m
                        src = w1nat[:, c, :] if c < K else w2nat_block(c - K)
                        mm = pe.transpose(o[:, m * P:(m + 1) * P], src, ident)
                mm.then_inc(s_wtp, 1)

            def prep_transpose(j, par):
                pe.wait_ge(s_zn, at(j, 1, 1))
                wait(pe, s_cT_sb, at(j, 1, 0))
                for t in range(TI):
                    mm = pe.transpose(pp[:, t * P:(t + 1) * P], zn[:, t, :], ident)
                mm.then_inc(s_zT, 1)

            def prep_logits(j, par):
                pe.wait_ge(s_zlo, at(j, 1, 1))
                pe.matmul(pp[:, :], rhi[:], zhi[:, par, :], start=True, stop=False)
                pe.matmul(pp[:, :], rlo[:], zhi[:, par, :], start=False, stop=False)
                pe.matmul(pp[:, :], rhi[:], zlo[:, par, :], start=False, stop=True).then_inc(s_lgT, 1)

            def prep_logits_back(j):
                pe.wait_ge(s_lgT_sb, at(j, 1, 1))
                for t in range(TI):
                    mm = pe.transpose(pp[:, t * P:(t + 1) * P], lgT[:, t * P:(t + 1) * P], ident)
                mm.then_inc(s_logit, 1)

            def prep_combine(j):
                pe.wait_ge(s_router, at(j, ROUTER_OPS, ROUTER_OPS))
                pe.transpose(pp[0:E * TI, 0:P], combine[:].rearrange("p g k t -> p (g k t)"), ident)\
                    .then_inc(s_cT, 1)

            def expert_up(i, par, k):
                if k == 0:
                    pe.wait_ge(s_zlo, at(i, 1, 1))
                wait(pe, s_hhi, at(i, K, k - 1))
                o = up[k % 2][:, :]
                pe.matmul(o, w1hi[:, k, :], zhi[:, par, :], start=True, stop=False)
                pe.matmul(o, w1lo[:, k, :], zhi[:, par, :], start=False, stop=False)
                pe.matmul(o, w1hi[:, k, :], zlo[:, par, :], start=False, stop=True).then_inc(s_up, 1)

            def expert_down(i, k):
                e, first = k // FC, k % FC == 0
                pe.wait_ge(s_hlo, at(i, K, k + 1))
                if first:
                    wait(pe, s_prod, at(i, E, e - 1))
                o = down[e % 2][:, :]
                pe.matmul(o, w2hi[:, k, :], hhi[:, k % RING, :], start=first, stop=False)
                pe.matmul(o, w2lo[:, k, :], hhi[:, k % RING, :], start=False, stop=False)
                pe.matmul(o, w2hi[:, k, :], hlo[:, k % RING, :], start=False, stop=not first)\
                    .then_inc(s_down, 1)

            def finish(i, par):
                pe.wait_ge(s_acc, at(i, E - 1, E - 1))
                pe.wait_ge(s_logit_sb, min(i + 3, SLOTS) if isinstance(i, int) else at(i, 1, 3))
                for t in range(TI):
                    mm = pe.transpose(pp[:, t * P:(t + 1) * P], acc[:, par, t * P:(t + 1) * P], ident)
                mm.then_inc(s_fin, 1)

            def ret_transpose(i):
                if isinstance(i, int) and i == 0:
                    pe.wait_ge(s_ln, 1)
                else:
                    pe.wait_ge(s_xt, at(i - 1, 16, 16))
                wait(pe, s_A, at(i, TB * G, 0))
                src = xall[:, 0] if isinstance(i, int) and i == 0 else xt
                for t in range(TB):
                    mm = pe.transpose(m0[:, t * P:(t + 1) * P], src[:, t, :], ident)
                mm.then_inc(s_xT, 1)

            def ret_qk(i):
                pe.wait_ge(s_xT_sb, at(i, 1, 1))
                pe.matmul(m1[:, 0:T], wT[:, 0, :], xT[:], start=True, stop=True)
                pe.matmul(m1[:, T:2 * T], wT[:, 1, :], xT[:], start=True, stop=True).then_inc(s_qk, 1)

            def ret_vk(i):
                for t in range(TB):
                    mm = pe.matmul(m0[:, t * T:(t + 1) * T], xT[:, t * P:(t + 1) * P],
                                   wT[:, 1:3, :].rearrange("p a n -> p (a n)"), start=True, stop=True)
                mm.then_inc(s_vk, 1)

            def ret_state(i):
                pe.wait_ge(s_k0, at(i, 1, 1))
                pe.wait_ge(s_v_sb, at(i, V_COPIES, V_COPIES))
                pe.wait_ge(s_qk_sb, at(i, QK_OPS, QK_OPS))
                pe.matmul(m1[:, 0:P], k0[:], v0[:], start=True, stop=True).then_inc(s_state, 1)

            def ret_score(i, t, g):
                o = (m0, m1)[g % 2]
                if t == 0 and g == 1:
                    pe.wait_ge(s_state_sb, at(i, 1, 1))
                n = t * G + g
                if n >= 2:
                    pe.wait_ge(s_A, at(i, TB * G, n - 1))
                rows = slice(32 * g, 32 * g + 32)
                pe.matmul(o[:, :], kT[rows, t * P:(t + 1) * P], qblk[rows, :, t * P:(t + 1) * P],
                          start=True, stop=True, tile_position=(32 * g, 0)).then_inc(s_score, 1)

            def ret_av(i, t):
                pe.wait_ge(s_A, at(i, TB * G, (t + 1) * G))
                o = yy[:, t * P:(t + 1) * P]
                if t == 0:
                    wait(pe, s_wo_sb, at(i, 1, 0))
                else:
                    pe.matmul(o, state[:], q1[:], start=True, stop=False, skip_group_check=True)
                for h in range(GH):
                    for g in range(G):
                        mm = pe.matmul(yy[32 * g:32 * g + 32, t * P:(t + 1) * P],
                                       vpad[:, t, g, h, :, :].rearrange("p a b -> p (a b)"),
                                       A[:, t, g, h, :], start=(t == 0 and h == 0), stop=(h == GH - 1),
                                       tile_position=(0, 32 * g), skip_group_check=True)
                mm.then_inc(s_av, 1)

            def ret_head_mean(i):
                pe.wait_ge(s_gn, at(i, GN_OPS, 6))
                pe.matmul(yy[:, T:T + 2], const_of("headmean"), ghm[:], start=True, stop=True)\
                    .then_inc(s_gn_ps, 1)

            def ret_out(i):
                pe.wait_ge(s_yn, at(i, 1, 1))
                for t in range(TB):
                    mm = pe.matmul(yy[:, T + t * P:T + (t + 1) * P], ynT[:, t * P:(t + 1) * P], wT[:, 3, :],
                                   start=True, stop=True)
                mm.then_inc(s_wo, 1)

            for n in range(4):
                weights(n)
            prep_transpose(0, 0)
            weights(4)
            weights(5)
            prep_logits(0, 0)
            weights(6)
            weights(7)
            prep_logits_back(0)
            weights(8)
            weights(9)
            prep_combine(0)
            pe.wait_ge(s_whi, WGROUPS)
            pe.wait_ge(s_wlo, WGROUPS - 1)
            pe.wait_ge(s_const, 16)

            def slot(i, par, first=False, second=False, last=False):
                for k in range(K):
                    expert_up(i, par, k)
                    if k >= LAG:
                        expert_down(i, k - LAG)
                    elif not first:
                        expert_down(i - 1, k - LAG + K)
                    if k == 0:
                        ret_transpose(i)
                    if k == 1:
                        ret_qk(i)
                    if k == 2:
                        ret_vk(i)
                    if k == 1 and not first:
                        ret_head_mean(i - 1)
                    if k == 4:
                        ret_state(i)
                    if k == 6 and not first:
                        ret_out(i - 1)
                    if not last:
                        if k == 3:
                            prep_transpose(i + 1, 1 - par)
                        if k == 5:
                            prep_logits(i + 1, 1 - par)
                        if k == 6:
                            prep_logits_back(i + 1)
                    if k == 9 and not first:
                        finish(i - 1, 1 - par)
                    if 5 <= k < 5 + TB * G:
                        ret_score(i, (k - 5) // G, (k - 5) % G)
                    if k == 10:
                        ret_av(i, 0)
                    if k == 14:
                        ret_av(i, 1)
                    if k == 13 and not last:
                        if not first:
                            pe.wait_ge(s_fin_sum, at(i, 1, 0))
                        prep_combine(i + 1)

            slots_of(pe, slot)
            for k in range(K - LAG, K):
                expert_down(SLOTS - 1, k)
            ret_head_mean(B - 1)
            ret_out(B - 1)
            finish(SLOTS - 1, 1)

        @block.scalar
        def _(act):
            act.dma_start(rnat[0:NG, :], w_macro).then_inc(s_rnat, 16)
            act.dma_start(rnat[NG:NR, :], w_micro.rearrange("g e d -> (g e) d")).then_inc(s_rnat, 16)
            act.dma_start(vecs[:, 0:1], norm_w.rearrange("(p o) -> p o", o=1)).then_inc(s_vecs, 16)
            act.dma_start(vecs[:, 1:2], gn_weight.rearrange("(p o) -> p o", o=1)).then_inc(s_vecs, 16)
            act.dma_start(vecs[:, 2:3], gn_bias.rearrange("(p o) -> p o", o=1)).then_inc(s_vecs, 16)
            act.dma_start(w1nat[:], w1.rearrange("e (c p) d -> p (e c) d", p=P)).then_inc(s_w1nat, 16)
            act.dma_start(w2nat, w2.rearrange("e d f -> d e f")).then_inc(s_w2nat, 16)

            def weights(n):
                act.wait_ge(s_wtp, n + 1)
                if n == 0:
                    dst, src = wT[:].rearrange("p a n -> p (a n)"), wbank[0][:, :]
                elif n == 1:
                    act.wait_ge(s_zero, 2)
                    dst, src = rhi[:, 0:NR], wbank[1][:, 0:NR]
                else:
                    c = (n - 2) * 4
                    dst = (w1hi[:, c:c + 4, :] if c < K else w2hi[:, c - K:c - K + 4, :])\
                        .rearrange("p a n -> p (a n)")
                    src = wbank[n % 4][:, :]
                act.activation(dst, src, ACT.Copy).then_inc(s_whi, 1)

            def prep_high(j, par):
                act.wait_ge(s_zT, at(j, 1, 1))
                wait(act, s_up, at(j, K, -K))
                act.activation(zhi[:, par, :], pp[:, :], ACT.Copy, scale=norm_col).then_inc(s_zhi, 1)

            def prep_logits(j):
                act.wait_ge(s_lgT, at(j, 1, 1))
                act.activation(lgT[:], pp[:, :], ACT.Copy).then_inc(s_lgT_sb, 1)

            def router_tanh(j):
                act.wait_ge(s_router, at(j, ROUTER_OPS, 5))
                act.activation(rt[:, 6, :], rt[:, 5, :], ACT.Tanh, scale=0.5).then_inc(s_tanh, 1)
                act.activation(rt[:, 7, :], rt[:, 3, :], ACT.Abs).then_inc(s_tanh, 1)
                act.wait_ge(s_tanh, at(j, 3, 2))
                act.activation(rt[:, 8, :], rt[:, 7, :], ACT.Tanh, scale=0.5).then_inc(s_tanh, 1)

            def prep_combine(j):
                act.wait_ge(s_cT, at(j, 1, 1))
                wait(act, s_c_stored, at(j, 16, 0))
                act.activation(combine_T[:], pp[0:E * TI, 0:P], ACT.Copy).then_inc(s_cT_sb, 1)

            def hidden(i, k):
                act.wait_ge(s_up, at(i, K, k + 1))
                wait(act, s_hlo, at(i, K, k + 1 - RING))
                act.activation(hf[:, k % RING, :], up[k % 2][:, :], ACT.Silu).then_inc(s_hf, 1)
                wait(act, s_down, at(i, K, k + 1 - RING))
                act.activation(hhi[:, k % RING, :], up[k % 2][:, :], ACT.Silu).then_inc(s_hhi, 1)

            def ret_xT(i):
                act.wait_ge(s_xT, at(i, 1, 1))
                wait(act, s_vk, at(i, 1, 0))
                act.activation(xT[:], m0[:, 0:T], ACT.Copy).then_inc(s_xT_sb, 1)

            def ret_v(i):
                act.wait_ge(s_vk, at(i, 1, 1))
                wait(act, s_av, at(i, TB, 0))
                for t in range(TB):
                    src = m0[:, t * T + P:(t + 1) * T].rearrange("p (g h d) -> p g h d", g=G, h=GH)
                    flat = vpad[:, t].rearrange("p g h a d -> p g (h a) d")[:, :, ::GH + 1, :]
                    act.activation(flat, src, ACT.Copy).then_inc(s_v_sb, 1)
                act.activation(v0[:], m0[:, P:T], ACT.Copy).then_inc(s_v_sb, 1)

            def ret_norm(i):
                act.wait_ge(s_gn, at(i, GN_OPS, GN_OPS))
                wait(act, s_wo, at(i, 1, 0))
                act.activation(ynT[:], yy[:, 0:T], ACT.Identity, scale=gv[:, 2:3], bias=gv[:, 3:4])\
                    .then_inc(s_yn, 1)

            for n in range(4):
                weights(n)
            act.wait_ge(s_vecs, 48)
            prep_high(0, 0)
            weights(4)
            weights(5)
            prep_logits(0)
            weights(6)
            weights(7)
            router_tanh(0)
            weights(8)
            weights(9)
            prep_combine(0)
            act.wait_ge(s_zero, 3)

            def slot(i, par, first=False, second=False, last=False):
                for k in range(K):
                    hidden(i, k)
                    if k == 0:
                        ret_xT(i)
                    if k == 2:
                        ret_v(i)
                    if k == 4 and not first:
                        ret_norm(i - 1)
                    if not last:
                        if k == 3:
                            prep_high(i + 1, 1 - par)
                        if k == 5:
                            prep_logits(i + 1)
                        if k == 8:
                            router_tanh(i + 1)
                        if k == 13:
                            prep_combine(i + 1)

            slots_of(act, slot)
            ret_norm(B - 1)

        @block.vector
        def _(dve):
            ops = LNT + 6

            def layernorm(c):
                def need(n):
                    dve.wait_ge(s_ln_step, at(c, ops, n))

                dve.wait_ge(s_xall[c], 16)
                for t in range(LNT):
                    dve.bn_stats(stats[:, c, t, :], xall[:, c, t, :]).then_inc(s_ln_step, 1)
                me, ve, mo, vo = (stats[:, c, :, f] for f in (1, 2, 4, 5))
                mean2, diff, v2, sq, var, mean = (ln[:, c, f, :] for f in range(6))
                need(LNT)
                dve.tensor_tensor(diff, me, mo, ALU.subtract).then_inc(s_ln_step, 1)
                dve.tensor_tensor(v2, ve, vo, ALU.add).then_inc(s_ln_step, 1)
                dve.tensor_tensor(mean2, me, mo, ALU.add).then_inc(s_ln_step, 1)
                need(LNT + 2)
                dve.tensor_tensor(sq, diff, diff, ALU.mult).then_inc(s_ln_step, 1)
                dve.tensor_scalar(v2, v2, 1.0 / D, LN_EPS, ALU.mult, ALU.add).then_inc(s_ln_step, 1)
                need(LNT + 5)
                dve.scalar_tensor_tensor(out=var, in0=sq, scalar=0.25, in1=v2, op0=ALU.mult, op1=ALU.add)\
                    .then_inc(s_ln_var, 1)
                dve.tensor_scalar(mean, mean2, 0.5, None, ALU.mult).then_inc(s_ln_step, 1)
                need(LNT + 6)
                dve.wait_ge(s_ln_pow, c + 1)
                for t in range(LNT):
                    last = dve.tensor_scalar(xall[:, c, t, :], xall[:, c, t, :], ln[:, c, 5, t:t + 1],
                                             ln[:, c, 0, t:t + 1], ALU.subtract, ALU.mult)
                last.then_inc(s_ln, 1)

            def weights(n):
                dve.wait_ge(s_whi, n + 1)
                c = (n - 2) * 4
                if n == 1:
                    dst, src, hi = rlo[:, 0:NR], wbank[1][:, 0:NR], rhi[:, 0:NR]
                else:
                    his, los = (w1hi, w1lo) if c < K else (w2hi, w2lo)
                    dst, hi = (a[:, c % K:c % K + 4, :].rearrange("p a n -> p (a n)") for a in (los, his))
                    src = wbank[n % 4][:, :]
                dve.tensor_tensor(dst, src, hi.bitcast(F32), ALU.subtract).then_inc(s_wlo, 1)

            dve.memset(rhi[:].bitcast(F32), 0.0).then_inc(s_zero, 1)
            dve.memset(rlo[:].bitcast(F32), 0.0).then_inc(s_zero, 1)
            dve.memset(vpad[:].rearrange("p t g h a d -> p (t g h a d)"), 0.0).then_inc(s_zero, 1)

            def prep_mean_square(j):
                dve.wait_ge(s_sq, at(j, 1, 1))
                dve.tensor_reduce(ms[:, 0, :], zn[:], AX_X, ALU.add).then_inc(s_ms, 1)
                dve.wait_ge(s_ms, at(j, 2, 1))
                dve.tensor_scalar(ms[:, 1, :], ms[:, 0, :], 1.0 / D, RMS_EPS, ALU.mult, ALU.add)\
                    .then_inc(s_ms, 1)

            def prep_low(j, par):
                dve.wait_ge(s_zhi, at(j, 1, 1))
                dve.scalar_tensor_tensor(out=zlo[:, par, :], in0=pp[:, :], scalar=norm_col,
                                         in1=zhi[:, par, :].bitcast(F32), op0=ALU.mult, op1=ALU.subtract)\
                    .then_inc(s_zlo, 1)

            def prep_logits(j):
                dve.wait_ge(s_logit, at(j, 1, 1))
                dve.tensor_copy(logit[:], pp[:, :].rearrange("p (t c) -> p t c", t=TI)[:, :, 0:NR])\
                    .then_inc(s_logit_sb, 1)

            def row(n):
                return rt[:, n, :].rearrange("p (t g) -> p t g", t=TI)

            def one(n):
                return rt[:, n, 0:TI]

            def wide(ap):
                return ap.unsqueeze(2).broadcast_to([P, TI, NG])

            def router(j, part):
                m = logit[:, :, 0:NG]
                u = logit[:, :, NG:NR].rearrange("p t (g k) -> p t g k", k=PG)

                def need(n):
                    dve.wait_ge(s_router, at(j, ROUTER_OPS, n))

                if part == 0:
                    dve.wait_ge(s_logit_sb, at(j, 1, 1))
                    dve.tensor_reduce(one(0), m, AX_X, ALU.max).then_inc(s_router, 1)
                    dve.tensor_tensor(beats[:, 0], m.unsqueeze(3).broadcast_to([P, TI, NG, NG]),
                                      m.unsqueeze(2).broadcast_to([P, TI, NG, NG]), ALU.is_gt)\
                        .then_inc(s_router, 1)
                    dve.tensor_tensor(row(3), u[:, :, :, 0], u[:, :, :, 1], ALU.subtract)\
                        .then_inc(s_router, 1)
                    dve.tensor_tensor(row(4), u[:, :, :, 0], u[:, :, :, 1], ALU.is_ge)\
                        .then_inc(s_router, 1)
                    need(1)
                    dve.tensor_tensor(row(5), m, wide(one(0)), ALU.subtract).then_inc(s_router, 1)
                    need(2)
                    early = const_of("earlier").rearrange("p (o i j) -> p o i j", o=1, i=NG)\
                        .broadcast_to([P, TI, NG, NG])
                    dve.tensor_tensor(beats[:, 1], beats[:, 0], early, ALU.mult).then_inc(s_router, 1)
                if part == 1:
                    need(6)
                    dve.tensor_tensor(beats[:, 2], beats[:, 1], beats[:, 1].rearrange("p t i j -> p t j i"),
                                      ALU.subtract).then_inc(s_router, 1)
                    need(7)
                    dve.tensor_reduce(row(9), beats[:, 2], AX_X, ALU.add).then_inc(s_router, 1)
                    need(8)
                    dve.tensor_tensor(row(10), row(9),
                                      const_of("wins_needed").unsqueeze(1).broadcast_to([P, TI, NG]),
                                      ALU.is_ge).then_inc(s_router, 1)
                if part == 2:
                    dve.wait_ge(s_tanh, at(j, 3, 3))
                    dve.tensor_scalar(row(11), row(6), -1.0, 1.0, ALU.mult, ALU.add)\
                        .then_inc(s_router, 1)
                    dve.tensor_scalar(row(12), row(8), 0.5, 0.5, ALU.mult, ALU.add)\
                        .then_inc(s_router, 1)
                    need(10)
                    dve.reciprocal(row(13), row(11)).then_inc(s_router, 1)
                    need(11)
                    dve.tensor_scalar(row(14), row(12), TOPK_EPS, None, ALU.add)\
                        .then_inc(s_router, 1)
                    need(12)
                    dve.scalar_tensor_tensor(out=rt[:, 15, :], in0=rt[:, 6, :], scalar=1.0,
                                             in1=rt[:, 13, :], op0=ALU.add, op1=ALU.mult)\
                        .then_inc(s_router, 1)
                if part == 3:
                    need(14)
                    dve.tensor_tensor(row(16), row(15), row(10), ALU.mult).then_inc(s_router, 1)
                    dve.tensor_reduce(one(17), row(15), AX_X, ALU.add).then_inc(s_router, 1)
                    need(15)
                    dve.tensor_reduce(one(18), row(16), AX_X, ALU.add).then_inc(s_router, 1)
                    dve.tensor_tensor(row(21), row(16), row(12), ALU.mult).then_inc(s_router, 1)
                    need(17)
                    dve.scalar_tensor_tensor(out=one(19), in0=one(17), scalar=TOPK_EPS, in1=one(18),
                                             op0=ALU.mult, op1=ALU.add).then_inc(s_router, 1)
                if part == 4:
                    need(19)
                    dve.tensor_tensor(row(20), row(14), wide(one(19)), ALU.mult).then_inc(s_router, 1)
                    need(20)
                    dve.reciprocal(row(22), row(20)).then_inc(s_router, 1)
                    need(21)
                    dve.tensor_tensor(row(23), row(21), row(22), ALU.mult).then_inc(s_router, 1)
                    need(22)
                    wait(dve, s_cT, at(j, 1, 0))
                    picked = combine[:].rearrange("p g k t -> p k t g")
                    dve.tensor_tensor(picked[:, 0], row(23), row(4), ALU.mult).then_inc(s_router, 1)
                    need(23)
                    dve.tensor_tensor(picked[:, 1], row(23), picked[:, 0], ALU.subtract)\
                        .then_inc(s_router, 1)

            def low(i, k):
                dve.wait_ge(s_hhi, at(i, K, k + 1))
                wait(dve, s_down, at(i, K, k + 1 - RING))
                dve.tensor_tensor(hlo[:, k % RING, :], hf[:, k % RING, :],
                                  hhi[:, k % RING, :].bitcast(F32), ALU.subtract).then_inc(s_hlo, 1)

            def weigh(i, par, e):
                dve.wait_ge(s_down, at(i, K, FC * (e + 1)))
                if e == 0:
                    dve.wait_ge(s_cbc, at(i, 16, 16))
                    dst = acc[:, par, :]
                else:
                    wait(dve, s_acc, at(i, E - 1, e - 2) if e >= 2 else at(i, E - 1, 0))
                    dst = prod[:, e % 2, :]
                dve.tensor_tensor(dst, down[e % 2][:, :], cbc[:, par, e, :], ALU.mult).then_inc(s_prod, 1)

            def finish(i, second):
                dve.wait_ge(s_fin, at(i, 1, 1))
                dve.wait_ge(s_base, at(i, 16, 16))
                dve.wait_ge(s_z_stored, (i + LNC) * 16)
                flat = res[:].rearrange("p t d -> p (t d)")
                dve.tensor_tensor(flat, pp[:, :], base[:].rearrange("p t d -> p (t d)"), ALU.add)\
                    .then_inc(s_fin_sum, 1)
                if second:
                    dve.wait_ge(s_fin_sum, at(i, 1, 1))
                    dve.wait_ge(s_xa_in, at(i - NI, 16, 16))
                    dve.tensor_tensor(flat, flat, xa_in[:].rearrange("p t d -> p (t d)"), ALU.add)\
                        .then_inc(s_fin_out, 1)

            def ret_qk(i):
                dve.wait_ge(s_qk, at(i, 1, 1))
                wait(dve, s_av, at(i, TB, 0))
                dve.tensor_tensor(qblk[:], m1[:, 0:T].unsqueeze(1).broadcast_to([P, GH, T]),
                                  const_of("qdecay").rearrange("p (h t) -> p h t", h=GH), ALU.mult)\
                    .then_inc(s_qk_sb, 1)
                dve.tensor_tensor(q1[:], m1[:, P:T], const_of("qdecay_plain"), ALU.mult).then_inc(s_qk_sb, 1)
                dve.tensor_tensor(kT[:], m1[:, T:2 * T], const_of("kdecay"), ALU.mult).then_inc(s_qk_sb, 1)

            def ret_k0(i):
                dve.wait_ge(s_v_sb, at(i, V_COPIES, V_COPIES))
                dve.tensor_tensor(k0[:], m0[:, 0:P], const_of("kdecay_tok"), ALU.mult).then_inc(s_k0, 1)

            def ret_state(i):
                dve.wait_ge(s_state, at(i, 1, 1))
                dve.tensor_tensor(state[:], m1[:, 0:P], const_of("headmask"), ALU.mult)\
                    .then_inc(s_state_sb, 1)

            def ret_mask(i, n):
                dve.wait_ge(s_score, at(i, TB * G, n + 1))
                t, g = n // G, n % G
                src = (m0, m1)[g % 2][:, :].rearrange("p (h q) -> p h q", h=GH)
                dve.tensor_tensor(A[:, t, g], src, const_of("causal").unsqueeze(1).broadcast_to([P, GH, P]),
                                  ALU.mult).then_inc(s_A, 1)

            def ret_stats(i):
                dve.wait_ge(s_av, at(i, TB, TB))
                dve.bn_stats(gst[:], yy[:, 0:T]).then_inc(s_gn, 1)
                dve.wait_ge(s_gn, at(i, GN_OPS, 1))
                me, ve, mo, vo = gst[:, 1:2], gst[:, 2:3], gst[:, 4:5], gst[:, 5:6]
                dve.tensor_scalar(ghm[:, 0:1], me, mo, 0.5, ALU.add, ALU.mult).then_inc(s_gn, 1)
                dve.tensor_tensor(gsq[:, 0:1], me, me, ALU.mult).then_inc(s_gn, 1)
                dve.tensor_scalar(gsq[:, 1:2], ve, vo, 1.0 / T, ALU.add, ALU.mult).then_inc(s_gn, 1)
                dve.wait_ge(s_gn, at(i, GN_OPS, 3))
                dve.scalar_tensor_tensor(out=gsq[:, 2:3], in0=mo, scalar=mo, in1=gsq[:, 0:1],
                                         op0=ALU.mult, op1=ALU.add).then_inc(s_gn, 1)
                dve.wait_ge(s_gn, at(i, GN_OPS, 5))
                dve.scalar_tensor_tensor(out=ghm[:, 1:2], in0=gsq[:, 2:3], scalar=0.5, in1=gsq[:, 1:2],
                                         op0=ALU.mult, op1=ALU.add).then_inc(s_gn, 1)

            def ret_var(i):
                dve.wait_ge(s_gn_ps, at(i, 1, 1))
                dve.tensor_copy(gmv[:], yy[:, T:T + 2]).then_inc(s_gn_mean, 1)
                dve.wait_ge(s_gn_mean, at(i, 1, 1))
                dve.tensor_tensor(gv[:, 0:1], gmv[:, 0:1], gmv[:, 0:1], ALU.mult).then_inc(s_gn, 1)
                dve.wait_ge(s_gn, at(i, GN_OPS, 7))
                dve.scalar_tensor_tensor(out=gv[:, 1:2], in0=gmv[:, 1:2], scalar=LN_EPS, in1=gv[:, 0:1],
                                         op0=ALU.add, op1=ALU.subtract).then_inc(s_gn, 1)

            def ret_affine(i):
                dve.wait_ge(s_gn_pow, at(i, 1, 1))
                dve.tensor_tensor(gv[:, 2:3], gst[:, 0:1], gnw_col, ALU.mult).then_inc(s_gn, 1)
                dve.wait_ge(s_gn, at(i, GN_OPS, 9))
                dve.tensor_tensor(gst[:, 1:2], gmv[:, 0:1], gv[:, 2:3], ALU.mult).then_inc(s_gn_ms, 1)
                dve.wait_ge(s_gn_ms, at(i, 1, 1))
                dve.tensor_tensor(gv[:, 3:4], gnb_col, gst[:, 1:2], ALU.subtract).then_inc(s_gn, 1)

            def ret_residual(i):
                dve.wait_ge(s_wo, at(i, 1, 1))
                dve.wait_ge(s_xres, at(i, 16, 16))
                wait(dve, s_xa_stored, at(i, 16, 0))
                dve.tensor_tensor(xa_out[:].rearrange("p t d -> p (t d)"), yy[:, T:2 * T],
                                  xres[:].rearrange("p t d -> p (t d)"), ALU.add).then_inc(s_wo_sb, 1)

            layernorm(0)
            prep_mean_square(0)
            dve.wait_ge(s_zero, 3)
            for n in range(1, 4):
                weights(n)
            dve.wait_ge(s_vecs, 48)
            prep_low(0, 0)
            weights(4)
            weights(5)
            layernorm(1)
            prep_logits(0)
            router(0, 0)
            weights(6)
            router(0, 1)
            weights(7)
            router(0, 2)
            weights(8)
            router(0, 3)
            weights(9)
            router(0, 4)
            layernorm(2)

            def slot(i, par, first=False, second=False, last=False):
                for k in range(K):
                    low(i, k)
                    if k % 2 == 0:
                        if k >= 4:
                            weigh(i, par, (k - 4) // 2)
                        elif not first:
                            weigh(i - 1, 1 - par, E - 2 + k // 2)
                    if k == 0 and not last:
                        prep_mean_square(i + 1)
                    if k == 1:
                        ret_qk(i)
                    if k == 2 and not first:
                        ret_var(i - 1)
                    if k == 4 and not first:
                        ret_affine(i - 1)
                    if k == 2:
                        ret_k0(i)
                    if k == 4:
                        ret_state(i)
                    if k == 3 and not last:
                        prep_low(i + 1, 1 - par)
                    if k == 7 and not first:
                        ret_residual(i - 1)
                    if 5 <= k < 5 + TB * G:
                        ret_mask(i, k - 5)
                    if not last:
                        if k == 6:
                            prep_logits(i + 1)
                        if 7 <= k < 12:
                            router(i + 1, k - 7)
                    if k == 9 and not first:
                        finish(i - 1, second)
                    if first and k >= 4 and k % 2 == 1 and LN_BEFORE + (k - 5) // 2 < LNC:
                        layernorm(LN_BEFORE + (k - 5) // 2)
                ret_stats(i)

            slots_of(dve, slot)
            ret_var(B - 1)
            ret_affine(B - 1)
            weigh(SLOTS - 1, 1, E - 2)
            weigh(SLOTS - 1, 1, E - 1)
            ret_residual(B - 1)
            finish(SLOTS - 1, True)

        @block.gpsimd
        def _(pool):
            half = const_of("minus_half")
            pool.wait_ge(s_const0, 16)

            def layernorm(c):
                pool.wait_ge(s_ln_var, c + 1)
                pool.wait_ge(s_ln_step, at(c, LNT + 6, LNT + 6))
                pool.tensor_tensor(ln[:, c, 0, :], ln[:, c, 4, :], half[:, 0:LNT], ALU.pow)\
                    .then_inc(s_ln_pow, 1)

            def source(j):
                return xall[:, j] if isinstance(j, int) and j < 2 else zt

            def prep_square(j):
                if isinstance(j, int) and j < 2:
                    pool.wait_ge(s_ln, j + 1)
                else:
                    pool.wait_ge(s_zt, at(j - 2, 16, 16))
                wait(pool, s_zT, at(j, 1, 0))
                pool.tensor_tensor(zn[:], source(j)[:], source(j)[:], ALU.mult).then_inc(s_sq, 1)

            def prep_norm(j):
                pool.wait_ge(s_ms, at(j, 2, 2))
                pool.tensor_tensor(rstd[:], ms[:, 1, :], half[:, 0:TI], ALU.pow).then_inc(s_rstd, 1)
                pool.wait_ge(s_rstd, at(j, 1, 1))
                pool.tensor_tensor(zn[:], source(j)[:], rstd[:].unsqueeze(2).broadcast_to([P, TI, D]), ALU.mult)\
                    .then_inc(s_zn, 1)

            def add(i, par, e):
                pool.wait_ge(s_prod, at(i, E, e + 1))
                if e > 1:
                    pool.wait_ge(s_acc, at(i, E - 1, e - 1))
                pool.tensor_tensor(acc[:, par, :], acc[:, par, :], prod[:, e % 2, :], ALU.add)\
                    .then_inc(s_acc, 1)

            layernorm(0)
            prep_square(0)
            prep_norm(0)
            for c in range(1, LN_BEFORE):
                layernorm(c)

            def group_norm(b):
                pool.wait_ge(s_gn, at(b, GN_OPS, 8))
                pool.tensor_tensor(gst[:, 0:1], gv[:, 1:2], half[:, 0:1], ALU.pow).then_inc(s_gn_pow, 1)

            def slot(i, par, first=False, second=False, last=False):
                if not last:
                    prep_square(i + 1)
                if not first:
                    add(i - 1, 1 - par, E - 2)
                if not last:
                    prep_norm(i + 1)
                if not first:
                    group_norm(i - 1)
                if not first:
                    add(i - 1, 1 - par, E - 1)
                for e in range(1, E - 2):
                    if first:
                        layernorm(LN_BEFORE + e - 1)
                    add(i, par, e)

            slots_of(pool, slot)
            group_norm(B - 1)
            add(SLOTS - 1, 1, E - 2)
            add(SLOTS - 1, 1, E - 1)


_INS = ["L0_attn_x", "L0_attn_W_q", "L0_attn_W_k", "L0_attn_W_v", "L0_attn_W_o", "L0_attn_gn_weight",
        "L0_attn_gn_bias", "L0_ffn_norm_w", "L0_ffn_w_macro", "L0_ffn_w_micro", "L0_ffn_w1", "L0_ffn_w2"]


def kernel(**inputs):
    import numpy as _np
    import concourse.bacc as _bacc
    from concourse import mybir as _mybir
    from concourse.bass_utils import run_bass_kernel_spmd as _run

    nc = _bacc.Bacc("TRN2", target_bir_lowering=False, num_devices=1)
    arrays, args = {}, []
    for name in _INS:
        a = _np.ascontiguousarray(inputs[name])
        arrays[f"in_{name}_dram"] = a
        args.append(nc.dram_tensor(f"in_{name}_dram", a.shape, _mybir.dt.from_np(a.dtype), kind="ExternalInput").ap())
    arrays["constants_dram"] = constants()
    args.append(nc.dram_tensor("constants_dram", (P, NCONST), F32, kind="ExternalInput").ap())
    args.append(nc.dram_tensor("out_0_dram", (B, T, D), F32, kind="ExternalOutput").ap())
    program(nc, *args)
    r = _run(nc, [arrays], core_ids=[0])
    return r.results[0]["out_0_dram"]
```

```python
from contextlib import ExitStack

import concourse.bass as bass
from concourse import mybir

F32 = mybir.dt.float32
F32R = mybir.dt.float32r
ALU = mybir.AluOpType
ACT = mybir.ActivationFunctionType
AX_X = mybir.AxisListType.X

P = 128
B, T, D = 16, 256, 128
H = 16
DH = D // H
GH = 4
G = H // GH
TB = T // P
ITEM = 512
TI = ITEM // P
NI = B * T // ITEM
SLOTS = 2 * NI
E = 8
NG, PG = 4, 2
F = 256
FC = F // P
K = E * FC
LAG = 3
SCORE_AT = 5
RING = 4
NR = NG + E
LN_EPS = 1e-5
RMS_EPS = 1e-6
TOPK_EPS = 1e-9
LNBUF = 4

CONST = {}
_at = 0
for _name, _w in (("ident", P), ("earlier", NG * NG), ("wins_needed", NG), ("minus_half", TI),
                  ("over_d", TI), ("rms_eps", TI), ("kdecay_tok", P), ("qdecay", P), ("headmask", P), ("headmean", P),
                  ("blockmask", GH), ("decay", H * P)):
    CONST[_name] = (_at, _at + _w)
    _at += _w
NCONST = _at
NFIRST = CONST["kdecay_tok"][0]
NSECOND = CONST["decay"][0]

WPROJ = 1 + K // 4
WGROUPS = 2 + 2 * K // 4
LN_OPS = TI + 6
DOWN_AT = (0, 4, 5, 7)
COMBINE_AT = 3
CBC_PARTS = 4
ROUTER_OPS = 24
ROUTER_PARTS = 15
ROUTER_AT = 7
V_COPIES = 3
GN_OPS = 13
COPIES = 3
ROWS = 32 * COPIES


def constants():
    import numpy as np

    c = np.zeros((P, NCONST), np.float32)

    def put(name, a):
        lo, hi = CONST[name]
        c[:, lo:hi] = np.asarray(a, np.float64).reshape(a.shape[0], -1)

    head = np.arange(P) // DH
    gamma = 1.0 - 2.0 ** (-5.0 - np.arange(H))
    g = gamma[head][:, None]
    put("ident", np.eye(P))
    same = (head[:, None] == head[None, :]).astype(float)
    put("headmask", same)
    put("headmean", same / DH)
    put("kdecay_tok", (g ** -np.arange(P)[None, :]).T)
    put("qdecay", g ** np.arange(P, T)[None, :] / np.sqrt(DH))
    ahead = np.arange(P)[None, :] - np.arange(P)[:, None]
    put("decay", np.where(ahead[:, None, :] >= 0,
                          gamma[None, :, None] ** np.maximum(ahead, 0)[:, None, :], 0.0) / np.sqrt(DH))
    put("blockmask", (head[:, None] % GH == np.arange(GH)[None, :]).astype(float))
    put("earlier", np.tile((np.arange(NG)[:, None] > np.arange(NG)[None, :]).astype(float)[None], (P, 1, 1)))
    put("wins_needed", np.tile(np.arange(NG)[None] - 1.0, (P, 1)))
    put("over_d", np.full((P, TI), 1.0 / D))
    put("rms_eps", np.full((P, TI), RMS_EPS))
    put("minus_half", np.full((P, TI), -0.5))
    return c


def at(i, per_slot, nth):
    return i * per_slot + nth


def down_groups(k):
    return sum(a <= k for a in DOWN_AT)


def block_of(n):
    return (n - 1 if n < WPROJ else n - WPROJ - 1) * 4


def wait(eng, sem, value):
    if isinstance(value, int) and value <= 0:
        return
    eng.wait_ge(sem, value)


def program(nc, x, w_q, w_k, w_v, w_o, gn_weight, gn_bias, norm_w, w_macro, w_micro, w1, w2, const, out):
    z_dram = nc.dram_tensor("z_rounds", (2 * NI * ITEM, D), F32, kind="Internal").ap()
    xa_dram = nc.dram_tensor("x_plus_attn", (B * T, D), F32, kind="Internal").ap()
    c_dram = nc.dram_tensor("combine", (SLOTS * E * TI, P), F32, kind="Internal").ap()
    x_rows = x.rearrange("b t d -> (b t) d")
    out_rows = out.rearrange("b t d -> (b t) d")

    def item_rows(rows, i):
        return rows[bass.ds(i * ITEM, ITEM), :].rearrange("(t p) d -> p t d", p=P)

    def batch_rows(rows, b):
        return rows[bass.ds(b * T, T), :].rearrange("(t p) d -> p t d", p=P)

    with ExitStack() as ctx:
        def sb(name, shape, dt=F32):
            return ctx.enter_context(nc.sbuf_tensor(name, shape, dt))

        def bank(name):
            return ctx.enter_context(nc.psum_tensor(name, [P, 512], F32))

        def sem(name):
            return ctx.enter_context(nc.semaphore(name))

        cst = sb("cst", [P, NCONST])

        def const_of(name):
            return cst[:, CONST[name][0]:CONST[name][1]]

        ident = const_of("ident")
        vecs = sb("vecs", [P, 3])
        norm_col, gnw_col, gnb_col = (vecs[:, n:n + 1] for n in range(3))
        wnat = sb("wnat", [P, 4, D])
        rnat = sb("rnat", [NR, D])
        spare = sb("spare", [P, 2])
        wpr_hi = sb("wpr_hi", [P, 3, D], F32R)
        wpr_lo = sb("wpr_lo", [P, 3, D], F32R)
        wo = sb("wo", [P, D])
        router_w = sb("router_w", [P, 2 * NR], F32R)
        w1hi = sb("w1hi", [P, K, P], F32R)
        w1lo = sb("w1lo", [P, K, P], F32R)
        w2hi = sb("w2hi", [P, K, P], F32R)
        w2lo = sb("w2lo", [P, K, P], F32R)
        xln = sb("xln", [P, LNBUF, TI, D])
        w1nat = sb("w1nat", [P, K, D])
        w2nat_sb = sb("w2nat", [P, E, F])
        w2nat = w2nat_sb[:]

        def w2nat_block(c):
            return w2nat_sb[:, c // FC, (c % FC) * P:(c % FC + 1) * P]

        stats = sb("stats", [P, TI, 6])
        ln = sb("ln", [P, 6, TI])
        zt = sb("zt", [P, TI, D])
        zn = sb("zn", [P, TI, D])
        ms = sb("ms", [P, 3, TI])
        rstd = sb("rstd", [P, TI])
        zhi = sb("zhi", [P, 2, ITEM], F32R)
        zlo = sb("zlo", [P, 2, ITEM], F32R)
        logit = sb("logit", [P, TI, NR])
        rt = sb("rt", [P, 24, TI * NG])
        beats = sb("beats", [P, 3, TI, NG, NG])
        combine = sb("combine_tok", [P, NG, PG, TI])
        combine_T = sb("combine_T", [E * TI, P])
        cbc = sb("cbc", [P, 2, E, ITEM])
        hf = sb("hf", [P, RING, ITEM])
        hhi = sb("hhi", [P, RING, ITEM], F32R)
        hlo = sb("hlo", [P, RING, ITEM], F32R)
        prod = sb("prod", [P, 2, ITEM])
        acc = sb("acc", [P, 2, ITEM])
        base = sb("base", [P, TI, D])
        xa_in = sb("xa_in", [P, TI, D])
        res = sb("res", [P, TI, D])
        xt = sb("xt", [P, TB, D])
        xres = sb("xres", [P, TB, D])
        xhi = sb("xhi", [P, T], F32R)
        xlo = sb("xlo", [P, T], F32R)
        split = sb("split", [P, COPIES, 2 * T], F32R)
        stack = sb("stack", [ROWS, G, 2 * T], F32R)
        qblk = sb("qblk", [ROWS, G, GH, T], F32R)
        q1 = sb("q1", [P, P])
        vpad = sb("vpad", [P, TB, G, GH, GH, DH])
        v0 = sb("v0", [P, P])
        k0 = sb("k0", [P, P])
        state = sb("state", [P, P])
        A = [w1nat[:].rearrange("p (g h) q -> p g h q", g=G),
             w2nat_sb[:].rearrange("p e (a q) -> p (e a) q", q=P).rearrange("p (g h) q -> p g h q", g=G)]
        gst = sb("gst", [P, 6])
        gsq = sb("gsq", [P, 4])
        gmv = sb("gmv", [P, 2])
        ghm = sb("ghm", [P, 2])
        gv = sb("gv", [P, 7])
        ynT = wnat[:, 0:2, :].rearrange("p a n -> p (a n)")
        xa_out = wnat[:, 2:4, :]

        up = [bank(f"up{n}") for n in range(2)]
        down = [bank(f"down{n}") for n in range(2)]
        m0, m1, pp, yy = bank("m0"), bank("m1"), bank("pp"), bank("yy")
        wbank = [yy, down[0], down[1], m0, m1]

        s_const0 = sem("s_const0")
        s_const = sem("s_const")
        s_decay = sem("s_decay")
        s_vecs = sem("s_vecs")
        s_vecs2 = sem("s_vecs2")
        s_wnat = sem("s_wnat")
        s_rnat = sem("s_rnat")
        s_w1nat = sem("s_w1nat")
        s_w2nat = sem("s_w2nat")
        s_xln = sem("s_xln")
        s_zt = sem("s_zt")
        s_xt = sem("s_xt")
        s_xres = sem("s_xres")
        s_base = sem("s_base")
        s_xa_in = sem("s_xa_in")
        s_cbc = sem("s_cbc")
        s_cbc_first = [sem(f"s_cbc_first{n}") for n in range(CBC_PARTS)]
        s_z_stored = sem("s_z_stored")
        s_piece_stored = sem("s_piece_stored")
        s_xa_stored = sem("s_xa_stored")
        s_c_stored = sem("s_c_stored")
        s_wtp = sem("s_wtp")
        s_whi = sem("s_whi")
        s_wlo = sem("s_wlo")
        s_ln = sem("s_ln")
        s_ln_step = sem("s_ln_step")
        s_ln_var = sem("s_ln_var")
        s_ln_pow = sem("s_ln_pow")
        s_ln_centred = sem("s_ln_centred")
        s_sq = sem("s_sq")
        s_ms = sem("s_ms")
        s_rstd = sem("s_rstd")
        s_zn = sem("s_zn")
        s_zT = sem("s_zT")
        s_zhi = sem("s_zhi")
        s_zlo = sem("s_zlo")
        s_logit = sem("s_logit")
        s_logit_sb = sem("s_logit_sb")
        s_router = sem("s_router")
        s_tanh = sem("s_tanh")
        s_cT = sem("s_cT")
        s_cT_sb = sem("s_cT_sb")
        s_up = sem("s_up")
        s_hhi = sem("s_hhi")
        s_hlo = sem("s_hlo")
        s_down = sem("s_down")
        s_prod = sem("s_prod")
        s_acc = sem("s_acc")
        s_fin = sem("s_fin")
        s_fin_sum = sem("s_fin_sum")
        s_fin_out = sem("s_fin_out")
        s_xT = sem("s_xT")
        s_xhi = sem("s_xhi")
        s_xlo = sem("s_xlo")
        s_proj = sem("s_proj")
        s_high = sem("s_high")
        s_low = sem("s_low")
        s_stack = [sem(f"s_stack{g}") for g in range(G)]
        s_qblk = sem("s_qblk")
        s_kvq = sem("s_kvq")
        s_v_sb = sem("s_v_sb")
        s_k0 = sem("s_k0")
        s_state = sem("s_state")
        s_state_sb = sem("s_state_sb")
        s_score = sem("s_score")
        s_A = sem("s_A")
        s_av = sem("s_av")
        s_gn = sem("s_gn")
        s_gn_ps = sem("s_gn_ps")
        s_gn_mean = sem("s_gn_mean")
        s_gn_stats = sem("s_gn_stats")
        s_yn = sem("s_yn")
        s_wo = sem("s_wo")
        s_wo_sb = sem("s_wo_sb")
        s_zero = sem("s_zero")
        s_zero_wide = sem("s_zero_wide")

        def bank_of(n):
            return wbank[n] if n < WPROJ else yy

        def z_of(j):
            return xln[:, j] if isinstance(j, int) and j < 2 else zt[:]

        def buf_of(c, par):
            return xln[:, c] if isinstance(c, int) else xln[:, 1 - par]

        def slots_of(eng, slot, pairs_alone=0):
            slot(0, 0, first=True)
            with eng.Fori(0, NI // 4) as it:
                slot(it * 2 + 1, 1, norm=True)
                slot(it * 2 + 2, 0, norm=True)
            with eng.Fori(NI // 4, NI // 2) as it:
                slot(it * 2 + 1, 1)
                slot(it * 2 + 2, 0)
            with eng.Fori(NI // 2, NI - 1 - pairs_alone) as it:
                slot(it * 2 + 1, 1, second=True)
                slot(it * 2 + 2, 0, second=True)
            for i in range(SLOTS - 1 - 2 * pairs_alone, SLOTS - 1):
                slot(i, i % 2, second=True)
            slot(SLOTS - 1, 1, second=True, last=True)

        block = ctx.enter_context(nc.Block())

        @block.sync
        def _(sp):
            def load_piece(c, par):
                sp.dma_start(buf_of(c, par), item_rows(x_rows, c)).then_inc(s_xln, 16)

            def store_piece(c, par):
                sp.wait_ge(s_ln, at(c, 1, 1))
                stored = s_z_stored if isinstance(c, int) and c == 0 else s_piece_stored
                sp.dma_start(item_rows(z_dram, c), buf_of(c, par)).then_inc(stored, 16)

            load_piece(0, 0)
            sp.dma_start(rnat[0:NG, :], w_macro).then_inc(s_rnat, 16)
            sp.dma_start(rnat[NG:NR, :], w_micro.rearrange("g e d -> (g e) d")).then_inc(s_rnat, 16)
            for n, w in enumerate((w_q, w_k, w_v, w_o)):
                sp.dma_start(wnat[:, n, :], w).then_inc(s_wnat, 16)
            sp.wait_ge(s_xln, 16)
            load_piece(1, 0)
            sp.dma_start(w2nat, w2.rearrange("e d f -> d e f")).then_inc(s_w2nat, 16)
            sp.dma_start(cst[:, NFIRST:NSECOND], const[:, NFIRST:NSECOND]).then_inc(s_const, 16)
            for c in (2, 3):
                sp.wait_ge(s_xln, at(c, 16, 0))
                load_piece(c, 0)
            sp.dma_start(vecs[:, 1:2], gn_weight.rearrange("(p o) -> p o", o=1)).then_inc(s_vecs2, 16)
            sp.dma_start(vecs[:, 2:3], gn_bias.rearrange("(p o) -> p o", o=1)).then_inc(s_vecs2, 16)
            sp.dma_start(cst[:, NSECOND:], const[:, NSECOND:]).then_inc(s_decay, 16)
            sp.dma_start(xres[:], batch_rows(x_rows, 0)).then_inc(s_xres, 16)
            store_piece(0, 0)

            def load_item(j):
                sp.wait_ge(s_zn, at(j, 1, 0))
                sp.dma_start(zt[:], item_rows(z_dram, j)).then_inc(s_zt, 16)

            def stack_group(b, g):
                wait(sp, s_score, at(b, TB * G, g + 1 - G))
                if g == 0:
                    sp.wait_ge(s_low, at(b, 1, 1))
                for c in range(COPIES):
                    rows, part = slice(32 * c, 32 * c + 32), split[32 * g:32 * g + 32, c, :]
                    sp.dma_start(stack[rows, g, :].bitcast(F32), part.bitcast(F32))\
                        .then_inc(s_stack[g], 16)

            def combine_rows(j):
                return c_dram[bass.ds(j * (E * TI), E * TI), :]

            def spread_store(j):
                sp.wait_ge(s_cT_sb, at(j, 1, 1))
                sp.dma_start(combine_rows(j), combine_T[:]).then_inc(s_c_stored, 16)

            def spread_load(j, par, prods, signals):
                wait(sp, s_prod, prods)
                sp.wait_ge(s_c_stored, (j + 1) * 16)
                flat = combine_rows(j).rearrange("(o r) p -> o (r p)", o=1)
                dst = cbc[:, par].rearrange("p e t -> p (e t)")
                step = E * ITEM // len(signals)
                for n, signal in enumerate(signals):
                    cols = slice(n * step, (n + 1) * step)
                    sp.dma_start(dst[:, cols], flat[:, cols].broadcast_to([P, step])).then_inc(signal, 16)

            for g in range(G):
                stack_group(0, g)
            spread_store(0)
            spread_load(0, 0, 0, s_cbc_first)
            store_piece(1, 0)

            def finish_loads(i, second):
                sp.dma_start(base[:], item_rows(z_dram, i)).then_inc(s_base, 16)
                if isinstance(i, int) and i == SLOTS - 1:
                    sp.wait_ge(s_xa_stored, (B - 1) * 16)
                    sp.dma_start(xa_in[:, 0:TB, :], batch_rows(xa_dram, B - 2)).then_inc(s_xa_in, 16)
                elif second:
                    sp.wait_ge(s_xa_stored, (i - NI) * 32 + 32)
                    sp.dma_start(xa_in[:], item_rows(xa_dram, i - NI)).then_inc(s_xa_in, 16)

            def finish_store(i, second):
                if second:
                    sp.wait_ge(s_fin_out, at(i - NI, 1, 1))
                else:
                    sp.wait_ge(s_fin_sum, at(i, 1, 1))
                dst = item_rows(out_rows, i - NI) if second else item_rows(z_dram, i + NI)
                sp.dma_start(dst, res[:]).then_inc(s_z_stored, 16)

            def store_retention(b):
                sp.wait_ge(s_wo_sb, at(b, 1, 1))
                sp.dma_start(batch_rows(xa_dram, b), xa_out).then_inc(s_xa_stored, 16)

            def slot(i, par, first=False, norm=False, second=False, last=False):
                if norm:
                    c = i + 3
                    sp.wait_ge(s_piece_stored, at(c, 16, -32))
                    load_piece(c, par)
                if not first:
                    finish_loads(i - 1, second)
                if not last:
                    sp.wait_ge(s_xT, at(i, 1, 1))
                    if first:
                        sp.wait_ge(s_z_stored, 16)
                    sp.dma_start(xt[:], batch_rows(z_dram, i + 1)).then_inc(s_xt, 16)
                if not first:
                    store_retention(i - 1)
                    sp.dma_start(xres[:], batch_rows(x_rows, i)).then_inc(s_xres, 16)
                if first:
                    store_piece(2, 0)
                    sp.wait_ge(s_piece_stored, 32)
                    load_item(2)
                elif norm:
                    j = i + 2
                    sp.wait_ge(s_piece_stored, at(j, 16, 0))
                    load_item(j)
                elif not last and not (isinstance(i, int) and i == SLOTS - 2):
                    j = i + 2
                    sp.wait_ge(s_piece_stored, 16 * (NI - 1))
                    sp.wait_ge(s_z_stored, at(j, 16, -32))
                    load_item(j)
                if not first:
                    finish_store(i - 1, second)
                if first:
                    store_piece(3, 0)
                if norm:
                    store_piece(i + 3, par)
                if not last:
                    stack_group(i + 1, 0)
                    spread_store(i + 1)
                    stack_group(i + 1, 1)
                    spread_load(i + 1, 1 - par, at(i, E, 0), [s_cbc])
                    stack_group(i + 1, 2)
                    stack_group(i + 1, 3)

            slots_of(sp, slot, pairs_alone=1)
            sp.wait_ge(s_fin_out, NI - 1)
            finish_loads(SLOTS - 1, True)
            finish_store(SLOTS - 1, True)
            sp.wait_ge(s_z_stored, 16 * (1 + SLOTS))
            sp.wait_ge(s_piece_stored, 16 * (NI - 1))
            sp.wait_ge(s_xa_stored, 16 * (B - 1))
            sp.wait_ge(s_c_stored, 16 * SLOTS)

        @block.tensor
        def _(pe):
            pe.wait_ge(s_const0, 16)

            def weights(n):
                o = bank_of(n)
                if n >= WPROJ:
                    pe.wait_ge(s_whi, n if n > WPROJ else 1)
                    pe.wait_ge(s_wlo, n if n > WPROJ else 1)
                if n == 0:
                    pe.wait_ge(s_rnat, 32)
                    mm = pe.transpose(o[:, 0:NR], rnat[:, :], ident[0:NR, 0:NR])
                elif n == WPROJ:
                    pe.wait_ge(s_wnat, 64)
                    for m in range(4):
                        mm = pe.transpose(o[:, m * P:(m + 1) * P], wnat[:, m, :], ident)
                else:
                    pe.wait_ge(s_w1nat if n < WPROJ else s_w2nat, 16)
                    for m in range(4):
                        c = block_of(n) + m
                        src = w1nat[:, c, :] if n < WPROJ else w2nat_block(c)
                        mm = pe.transpose(o[:, m * P:(m + 1) * P], src, ident)
                mm.then_inc(s_wtp, 1)

            def prep_transpose(j, par):
                pe.wait_ge(s_zn, at(j, 1, 1))
                if not (isinstance(j, int) and j == 0):
                    pe.wait_ge(s_v_sb, at(j, V_COPIES, 0))
                    pe.wait_ge(s_k0, at(j, 2, 0))
                for t in range(TI):
                    mm = pe.transpose(pp[:, t * P:(t + 1) * P], zn[:, t, :], ident)
                mm.then_inc(s_zT, 1)

            def prep_logits(j, par):
                pe.wait_ge(s_zlo, at(j, 1, 1))
                for t in range(TI):
                    toks = slice(t * P, (t + 1) * P)
                    pe.matmul(pp[:, t * P:t * P + 2 * NR], zhi[:, par, toks], router_w[:],
                              start=True, stop=False, skip_group_check=True)
                    mm = pe.matmul(pp[:, t * P:t * P + NR], zlo[:, par, toks], router_w[:, 0:NR],
                                   start=False, stop=True, skip_group_check=True)
                mm.then_inc(s_logit, 1)

            def prep_combine(j, o):
                pe.wait_ge(s_router, at(j, ROUTER_OPS, ROUTER_OPS))
                pe.transpose(o[0:E * TI, 0:P], combine[:].rearrange("p g k t -> p (g k t)"), ident)\
                    .then_inc(s_cT, 1)

            def expert_up(i, par, k):
                if k == 0:
                    pe.wait_ge(s_zlo, at(i, 1, 1))
                wait(pe, s_hhi, at(i, K, k - 1))
                o = up[k % 2][:, :]
                pe.matmul(o, w1hi[:, k, :], zhi[:, par, :], start=True, stop=False)
                pe.matmul(o, w1lo[:, k, :], zhi[:, par, :], start=False, stop=False)
                pe.matmul(o, w1hi[:, k, :], zlo[:, par, :], start=False, stop=True).then_inc(s_up, 1)

            def expert_down(i, k):
                e, first = k // FC, k % FC == 0
                pe.wait_ge(s_hlo, at(i, K, k + 1))
                if first:
                    wait(pe, s_prod, at(i, E, e - 1))
                o = down[e % 2][:, :]
                pe.matmul(o, w2hi[:, k, :], hhi[:, k % RING, :], start=first, stop=False)
                pe.matmul(o, w2lo[:, k, :], hhi[:, k % RING, :], start=False, stop=False)
                pe.matmul(o, w2hi[:, k, :], hlo[:, k % RING, :], start=False, stop=not first)\
                    .then_inc(s_down, 1)

            def finish(i, par):
                pe.wait_ge(s_acc, at(i, E - 1, E - 1))
                pe.wait_ge(s_logit_sb, min(i + 3, SLOTS) if isinstance(i, int) else at(i, 1, 3))
                for t in range(TI):
                    mm = pe.transpose(pp[:, t * P:(t + 1) * P], acc[:, par, t * P:(t + 1) * P], ident)
                mm.then_inc(s_fin, 1)

            def ret_transpose(i, o):
                if isinstance(i, int) and i == 0:
                    pe.wait_ge(s_ln, 1)
                else:
                    pe.wait_ge(s_xt, at(i - 1, 16, 16))
                if isinstance(i, int) and i == 1:
                    pe.wait_ge(s_whi, WGROUPS)
                    pe.wait_ge(s_wlo, WGROUPS)
                elif not (isinstance(i, int) and i == 0):
                    pe.wait_ge(s_wo_sb, at(i - 1, 1, 0))
                src = xln[:, 0] if isinstance(i, int) and i == 0 else xt
                for t in range(TB):
                    mm = pe.transpose(o[:, t * P:(t + 1) * P], src[:, t, :], ident)
                mm.then_inc(s_xT, 1)

            def split_product(o, w_hi, w_lo, m_hi, m_lo):
                pe.matmul(o, w_hi, m_hi, start=True, stop=False, skip_group_check=True)
                pe.matmul(o, w_lo, m_hi, start=False, stop=False, skip_group_check=True)
                return pe.matmul(o, w_hi, m_lo, start=False, stop=True, skip_group_check=True)

            def ret_kvq(i):
                if isinstance(i, int) and i == 0:
                    pe.wait_ge(s_logit_sb, 1)
                else:
                    pe.wait_ge(s_cT_sb, at(i, 1, 1))
                kv_hi, kv_lo = (w[:, 1:3, :].rearrange("p a n -> p (a n)") for w in (wpr_hi, wpr_lo))
                split_product(pp[:, 0:2 * P], xhi[:, 0:P], xlo[:, 0:P], kv_hi, kv_lo)
                split_product(pp[:, 2 * P:3 * P], xhi[:, P:T], xlo[:, P:T], wpr_hi[:, 2, :], wpr_lo[:, 2, :])
                split_product(pp[:, 3 * P:4 * P], wpr_hi[:, 0, :], wpr_lo[:, 0, :], xhi[:, P:T], xlo[:, P:T])\
                    .then_inc(s_kvq, 1)

            def ret_proj(i, o):
                pe.wait_ge(s_xlo, at(i, 1, 1))
                if isinstance(i, int) and i == 0:
                    pe.wait_ge(s_whi, WPROJ + 1)
                    pe.wait_ge(s_wlo, WPROJ + 1)
                elif isinstance(i, int) and i == 1:
                    pe.wait_ge(s_logit_sb, 2)
                else:
                    pe.wait_ge(s_fin_sum, at(i - 1, 1, 0))
                split_product(o[:, 0:T], wpr_hi[:, 0, :], wpr_lo[:, 0, :], xhi[:], xlo[:])
                split_product(o[:, T:2 * T], wpr_hi[:, 1, :], wpr_lo[:, 1, :], xhi[:], xlo[:]).then_inc(s_proj, 1)

            def ret_state(i):
                pe.wait_ge(s_k0, at(i, 2, 2))
                pe.wait_ge(s_v_sb, at(i, V_COPIES, V_COPIES))
                if isinstance(i, int) and i == B - 1:
                    pe.wait_ge(s_wo_sb, i)
                else:
                    pe.wait_ge(s_xlo, at(i, 1, 2))
                pe.matmul(yy[:, T:T + P], k0[:], v0[:], start=True, stop=True).then_inc(s_state, 1)

            def ret_score(i, t, g):
                n = t * G + g
                if t == 0:
                    pe.wait_ge(s_qblk, at(i, G, g + 1))
                wait(pe, s_A, at(i, TB * G, n - 1))
                pe.matmul((m1, m0)[g % 2][:, :], stack[:, g, T + t * P:T + (t + 1) * P],
                          qblk[:, g, :, t * P:(t + 1) * P], start=True, stop=True).then_inc(s_score, 1)

            def ret_av(i, t):
                pe.wait_ge(s_A, at(i, TB * G, (t + 1) * G))
                o = yy[:, t * P:(t + 1) * P]
                if t == 0:
                    pe.wait_ge(s_state_sb, at(i, 1, 1))
                else:
                    pe.matmul(o, state[:], q1[:], start=True, stop=False, skip_group_check=True)
                for h in range(GH):
                    for g in range(G):
                        mm = pe.matmul(yy[32 * g:32 * g + 32, t * P:(t + 1) * P],
                                       vpad[:, t, g, h, :, :].rearrange("p a b -> p (a b)"),
                                       A[t][:, g, h, :], start=(t == 0 and h == 0), stop=(h == GH - 1),
                                       tile_position=(0, 32 * g), skip_group_check=True)
                mm.then_inc(s_av, 1)

            def ret_head_mean(i):
                pe.wait_ge(s_gn, at(i, GN_OPS, 6))
                pe.matmul(yy[:, T:T + 2], const_of("headmean"), ghm[:], start=True, stop=True)\
                    .then_inc(s_gn_ps, 1)

            def ret_out(i):
                pe.wait_ge(s_yn, at(i, 1, 1))
                for t in range(TB):
                    mm = pe.matmul(yy[:, T + t * P:T + (t + 1) * P], ynT[:, t * P:(t + 1) * P], wo[:],
                                   start=True, stop=True)
                mm.then_inc(s_wo, 1)

            for n in range(WPROJ):
                weights(n)
            prep_transpose(0, 0)
            weights(WPROJ)
            pe.wait_ge(s_whi, WPROJ)
            pe.wait_ge(s_wlo, WPROJ)
            ret_transpose(0, m0)
            ret_proj(0, m1)

            def slot(i, par, first=False, norm=False, second=False, last=False):
                for k in range(K):
                    expert_up(i, par, k)
                    if k >= LAG:
                        if first and (k - LAG) % 4 == 0:
                            pe.wait_ge(s_wlo, WPROJ + 2 + (k - LAG) // 4)
                        expert_down(i, k - LAG)
                    elif not first:
                        expert_down(i - 1, k - LAG + K)
                    if first:
                        if k == 0:
                            prep_logits(0, 0)
                        if k == COMBINE_AT + 1:
                            pe.wait_ge(s_cT_sb, 1)
                        if k in DOWN_AT:
                            weights(WPROJ + 1 + DOWN_AT.index(k))
                        if k == COMBINE_AT:
                            pe.wait_ge(s_whi, WPROJ + 1 + down_groups(k))
                            pe.wait_ge(s_wlo, WPROJ + 1 + down_groups(k))
                            prep_combine(0, yy)
                    if k == (2 if first else 1):
                        ret_kvq(i)
                    if k == 2 and not first:
                        ret_head_mean(i - 1)
                    if k == 6 and not first:
                        ret_out(i - 1)
                    if k == 11:
                        ret_state(i)
                    if not last:
                        if k == 9:
                            ret_transpose(i + 1, yy)
                        if k == 12:
                            ret_proj(i + 1, pp)
                        if k == 3:
                            prep_transpose(i + 1, 1 - par)
                        if k == 5:
                            prep_logits(i + 1, 1 - par)
                    if k == 8 and not first:
                        finish(i - 1, 1 - par)
                    if SCORE_AT <= k < SCORE_AT + TB * G:
                        ret_score(i, (k - SCORE_AT) // G, (k - SCORE_AT) % G)
                    if k == 13:
                        ret_av(i, 0)
                    if k == 15 and not last:
                        pe.wait_ge(s_low, at(i, 1, 2))
                        prep_combine(i + 1, pp)
                    if k == (14 if last else 15):
                        ret_av(i, 1)

            slots_of(pe, slot)
            for k in range(K - LAG, K):
                expert_down(SLOTS - 1, k)
                if k == K - 2:
                    ret_head_mean(B - 1)
            ret_out(B - 1)
            finish(SLOTS - 1, 1)

        @block.scalar
        def _(act):
            act.dma_start(cst[:, 0:NFIRST], const[:, 0:NFIRST]).then_inc(s_const0, 16)
            act.dma_start(w1nat[:], w1.rearrange("e (c p) d -> p (e c) d", p=P)).then_inc(s_w1nat, 16)
            act.dma_start(vecs[:, 0:1], norm_w.rearrange("(p o) -> p o", o=1)).then_inc(s_vecs, 16)
            def weights(n):
                act.wait_ge(s_wtp, n + 1)
                if n == 0:
                    dst, src = router_w[:, 0:NR], wbank[0][:, 0:NR]
                elif n == WPROJ:
                    src = bank_of(n)
                    act.activation(wo[:], src[:, 3 * P:], ACT.Copy)
                    dst, src = wpr_hi[:].rearrange("p a n -> p (a n)"), src[:, 0:3 * P]
                else:
                    c = block_of(n)
                    dst = (w1hi if n < WPROJ else w2hi)[:, c:c + 4, :].rearrange("p a n -> p (a n)")
                    src = bank_of(n)[:, :]
                act.activation(dst, src, ACT.Copy).then_inc(s_whi, 1)

            def prep_square(j):
                if isinstance(j, int) and j < 2:
                    act.wait_ge(s_ln, j + 1)
                else:
                    act.wait_ge(s_zt, at(j - 2, 16, 16))
                wait(act, s_zT, at(j, 1, 0))
                for t in range(TI):
                    last = act.activation(zn[:, t, :], z_of(j)[:, t, :], ACT.Square, accum_out=ms[:, 0, t:t + 1])
                last.then_inc(s_sq, 1)

            def prep_high(j, par):
                act.wait_ge(s_zT, at(j, 1, 1))
                wait(act, s_up, at(j, K, -K))
                act.activation(zhi[:, par, :], pp[:, :], ACT.Copy, scale=norm_col).then_inc(s_zhi, 1)

            def router_tanh(j):
                act.wait_ge(s_router, at(j, ROUTER_OPS, 5))
                act.activation(rt[:, 6, :], rt[:, 5, :], ACT.Tanh, scale=0.5).then_inc(s_tanh, 1)
                act.activation(rt[:, 7, :], rt[:, 3, :], ACT.Abs).then_inc(s_tanh, 1)
                act.wait_ge(s_tanh, at(j, 3, 2))
                act.activation(rt[:, 8, :], rt[:, 7, :], ACT.Tanh, scale=0.5).then_inc(s_tanh, 1)

            def prep_combine(j, src):
                act.wait_ge(s_cT, at(j, 1, 1))
                wait(act, s_c_stored, at(j, 16, 0))
                act.activation(combine_T[:], src[0:E * TI, 0:P], ACT.Copy).then_inc(s_cT_sb, 1)

            def hidden(i, k):
                act.wait_ge(s_up, at(i, K, k + 1))
                wait(act, s_hlo, at(i, K, k + 1 - RING))
                act.activation(hf[:, k % RING, :], up[k % 2][:, :], ACT.Silu)
                wait(act, s_down, at(i, K, k + 1 - RING))
                act.activation(hhi[:, k % RING, :], up[k % 2][:, :], ACT.Silu).then_inc(s_hhi, 1)

            def ret_xT(i, src):
                act.wait_ge(s_xT, at(i, 1, 1))
                wait(act, s_kvq, at(i, 1, 0))
                act.activation(xhi[:], src[:, 0:T], ACT.Copy).then_inc(s_xhi, 1)

            def ret_high(i, src):
                act.wait_ge(s_proj, at(i, 1, 1))
                for g in range(G):
                    wait(act, s_stack[g], at(i, 16 * COPIES, 0))
                act.activation(split[:, 0, :], src[:, :], ACT.Copy)
                act.activation(split[:, 1, 0:T], src[:, 0:T], ACT.Copy)
                act.activation(split[:, 2, T:], src[:, T:], ACT.Copy).then_inc(s_high, 1)

            def ret_v(i):
                act.wait_ge(s_kvq, at(i, 1, 1))
                wait(act, s_av, at(i, TB, 0))
                for t in range(TB):
                    src = pp[:, (t + 1) * P:(t + 2) * P].rearrange("p (g h d) -> p g h d", g=G, h=GH)
                    flat = vpad[:, t].rearrange("p g h a d -> p g (h a) d")[:, :, ::GH + 1, :]
                    act.activation(flat, src, ACT.Copy).then_inc(s_v_sb, 1)
                act.activation(v0[:], pp[:, P:2 * P], ACT.Copy).then_inc(s_v_sb, 1)

            def ret_mean(i):
                act.wait_ge(s_gn_ps, at(i, 1, 1))
                wait(act, s_gn, at(i, GN_OPS, 0))
                act.activation(gmv[:], yy[:, T:T + 2], ACT.Copy, scale=0.5).then_inc(s_gn_mean, 1)

            def ret_norm(i):
                act.wait_ge(s_gn, at(i, GN_OPS, GN_OPS))
                wait(act, s_wo, at(i, 1, 0))
                act.activation(ynT, yy[:, 0:T], ACT.Identity, scale=gv[:, 2:3], bias=gv[:, 3:4])\
                    .then_inc(s_yn, 1)

            act.wait_ge(s_zero, 1)
            act.activation(spare[:, 1:2], spare[:, 0:1], ACT.Silu)
            weights(0)
            prep_square(0)
            for n in range(1, WPROJ):
                weights(n)
            act.wait_ge(s_vecs, 16)
            prep_high(0, 0)
            weights(WPROJ)
            ret_xT(0, m0)
            ret_high(0, m1)
            act.wait_ge(s_zero_wide, 1)

            def slot(i, par, first=False, norm=False, second=False, last=False):
                for k in range(K):
                    hidden(i, k)
                    if first:
                        if k in DOWN_AT:
                            weights(WPROJ + 1 + DOWN_AT.index(k))
                        if k == 1:
                            router_tanh(0)
                        if k == COMBINE_AT:
                            prep_combine(0, yy)
                    if k == 0 and first:
                        prep_square(1)
                    if k == 13 and not (isinstance(i, int) and i >= SLOTS - 2):
                        prep_square(i + 2)
                    if k == (2 if first else 1):
                        ret_v(i)
                    if k == 2 and not first:
                        ret_mean(i - 1)
                    if k == 4 and not first:
                        ret_norm(i - 1)
                    if not last:
                        if k == 3:
                            prep_high(i + 1, 1 - par)
                        if k == 8:
                            router_tanh(i + 1)
                        if k == 15:
                            prep_combine(i + 1, pp)
                        if k == 9:
                            ret_xT(i + 1, yy)
                        if k == 12:
                            ret_high(i + 1, pp)

            slots_of(act, slot, pairs_alone=1)
            ret_mean(B - 1)
            ret_norm(B - 1)

        @block.vector
        def _(dve):
            def layernorm_stats(c, par):
                def need(n):
                    dve.wait_ge(s_ln_step, at(c, LN_OPS, n))

                x = buf_of(c, par)
                dve.wait_ge(s_xln, at(c, 16, 16))
                if not (isinstance(c, int) and c <= 1):
                    dve.wait_ge(s_ln, at(c, 1, 0))
                for t in range(TI):
                    dve.bn_stats(stats[:, t, :], x[:, t, :]).then_inc(s_ln_step, 1)
                me, ve, mo, vo = (stats[:, :, f] for f in (1, 2, 4, 5))
                mean2, diff, v2, sq, var, mean = (ln[:, f, :] for f in range(6))
                need(TI)
                dve.tensor_tensor(diff, me, mo, ALU.subtract).then_inc(s_ln_step, 1)
                dve.tensor_tensor(v2, ve, vo, ALU.add).then_inc(s_ln_step, 1)
                dve.tensor_tensor(mean2, me, mo, ALU.add).then_inc(s_ln_step, 1)
                need(TI + 2)
                dve.tensor_tensor(sq, diff, diff, ALU.mult).then_inc(s_ln_step, 1)
                dve.tensor_scalar(v2, v2, 1.0 / D, LN_EPS, ALU.mult, ALU.add).then_inc(s_ln_step, 1)
                need(TI + 5)
                dve.scalar_tensor_tensor(out=var, in0=sq, scalar=0.25, in1=v2, op0=ALU.mult, op1=ALU.add)\
                    .then_inc(s_ln_var, 1)
                dve.tensor_scalar(mean, mean2, 0.5, None, ALU.mult).then_inc(s_ln_step, 1)

            def layernorm_apply(c, par):
                x = buf_of(c, par)
                dve.wait_ge(s_ln_step, at(c, LN_OPS, LN_OPS))
                dve.wait_ge(s_ln_pow, at(c, 1, 1))
                for t in range(TI):
                    last = dve.tensor_scalar(x[:, t, :], x[:, t, :], ln[:, 5, t:t + 1],
                                             ln[:, 0, t:t + 1], ALU.subtract, ALU.mult)
                last.then_inc(s_ln, 1)

            def weights(n):
                dve.wait_ge(s_whi, n + 1)
                if n == WPROJ:
                    dst, hi = (w[:].rearrange("p a n -> p (a n)") for w in (wpr_lo, wpr_hi))
                    src = bank_of(n)[:, 0:3 * P]
                elif n == 0:
                    dst, src, hi = router_w[:, NR:], wbank[0][:, 0:NR], router_w[:, 0:NR]
                else:
                    c = block_of(n)
                    his, los = (w1hi, w1lo) if n < WPROJ else (w2hi, w2lo)
                    dst, hi = (a[:, c:c + 4, :].rearrange("p a n -> p (a n)") for a in (los, his))
                    src = bank_of(n)[:, :]
                dve.tensor_tensor(dst, src, hi.bitcast(F32), ALU.subtract).then_inc(s_wlo, 1)

            dve.memset(spare[:], 0.0).then_inc(s_zero, 1)

            def prep_low(j, par):
                dve.wait_ge(s_zhi, at(j, 1, 1))
                dve.scalar_tensor_tensor(out=zlo[:, par, :], in0=pp[:, :], scalar=norm_col,
                                         in1=zhi[:, par, :].bitcast(F32), op0=ALU.mult, op1=ALU.subtract)\
                    .then_inc(s_zlo, 1)

            def prep_logits(j):
                dve.wait_ge(s_logit, at(j, 1, 1))
                both = pp[:, :].rearrange("p (t c) -> p t c", t=TI)
                dve.tensor_reduce(logit[:], both[:, :, 0:2 * NR].rearrange("p t (s r) -> p t r s", s=2), AX_X,
                                  ALU.add).then_inc(s_logit_sb, 1)

            def row(n):
                return rt[:, n, :].rearrange("p (t g) -> p t g", t=TI)

            def one(n):
                return rt[:, n, 0:TI]

            def wide(ap):
                return ap.unsqueeze(2).broadcast_to([P, TI, NG])

            def router(j, part):
                m = logit[:, :, 0:NG]
                u = logit[:, :, NG:NR].rearrange("p t (g k) -> p t g k", k=PG)
                picked = combine[:].rearrange("p g k t -> p k t g")

                def need(n):
                    dve.wait_ge(s_router, at(j, ROUTER_OPS, n))

                if part == 0:
                    dve.wait_ge(s_logit_sb, at(j, 1, 1))
                    dve.tensor_reduce(one(0), m, AX_X, ALU.max).then_inc(s_router, 1)
                    dve.tensor_tensor(beats[:, 0], m.unsqueeze(3).broadcast_to([P, TI, NG, NG]),
                                      m.unsqueeze(2).broadcast_to([P, TI, NG, NG]), ALU.is_gt)\
                        .then_inc(s_router, 1)
                    dve.tensor_tensor(row(3), u[:, :, :, 0], u[:, :, :, 1], ALU.subtract)\
                        .then_inc(s_router, 1)
                    dve.tensor_tensor(row(4), u[:, :, :, 0], u[:, :, :, 1], ALU.is_ge)\
                        .then_inc(s_router, 1)
                    need(1)
                    dve.tensor_tensor(row(5), m, wide(one(0)), ALU.subtract).then_inc(s_router, 1)
                    need(2)
                    early = const_of("earlier").rearrange("p (o i j) -> p o i j", o=1, i=NG)\
                        .broadcast_to([P, TI, NG, NG])
                    dve.tensor_tensor(beats[:, 1], beats[:, 0], early, ALU.mult).then_inc(s_router, 1)
                if part == 1:
                    need(6)
                    dve.tensor_tensor(beats[:, 2], beats[:, 1], beats[:, 1].rearrange("p t i j -> p t j i"),
                                      ALU.subtract).then_inc(s_router, 1)
                if part == 2:
                    need(7)
                    dve.tensor_reduce(row(9), beats[:, 2], AX_X, ALU.add).then_inc(s_router, 1)
                if part == 3:
                    need(8)
                    dve.tensor_tensor(row(10), row(9),
                                      const_of("wins_needed").unsqueeze(1).broadcast_to([P, TI, NG]),
                                      ALU.is_ge).then_inc(s_router, 1)
                if part == 4:
                    dve.wait_ge(s_tanh, at(j, 3, 3))
                    dve.tensor_scalar(row(11), row(6), -1.0, 1.0, ALU.mult, ALU.add)\
                        .then_inc(s_router, 1)
                    dve.tensor_scalar(row(12), row(8), 0.5, 0.5, ALU.mult, ALU.add)\
                        .then_inc(s_router, 1)
                if part == 5:
                    need(10)
                    dve.reciprocal(row(13), row(11)).then_inc(s_router, 1)
                    need(11)
                    dve.tensor_scalar(row(14), row(12), TOPK_EPS, None, ALU.add)\
                        .then_inc(s_router, 1)
                if part == 6:
                    need(12)
                    dve.scalar_tensor_tensor(out=rt[:, 15, :], in0=rt[:, 6, :], scalar=1.0,
                                             in1=rt[:, 13, :], op0=ALU.add, op1=ALU.mult)\
                        .then_inc(s_router, 1)
                if part == 7:
                    need(14)
                    dve.tensor_tensor(row(16), row(15), row(10), ALU.mult).then_inc(s_router, 1)
                    dve.tensor_reduce(one(17), row(15), AX_X, ALU.add).then_inc(s_router, 1)
                if part == 8:
                    need(15)
                    dve.tensor_reduce(one(18), row(16), AX_X, ALU.add).then_inc(s_router, 1)
                    dve.tensor_tensor(row(21), row(16), row(12), ALU.mult).then_inc(s_router, 1)
                if part == 9:
                    need(17)
                    dve.scalar_tensor_tensor(out=one(19), in0=one(17), scalar=TOPK_EPS, in1=one(18),
                                             op0=ALU.mult, op1=ALU.add).then_inc(s_router, 1)
                if part == 10:
                    need(19)
                    dve.tensor_tensor(row(20), row(14), wide(one(19)), ALU.mult).then_inc(s_router, 1)
                if part == 11:
                    need(20)
                    dve.reciprocal(row(22), row(20)).then_inc(s_router, 1)
                if part == 12:
                    need(21)
                    dve.tensor_tensor(row(23), row(21), row(22), ALU.mult).then_inc(s_router, 1)
                if part == 13:
                    need(22)
                    wait(dve, s_cT, at(j, 1, 0))
                    dve.tensor_tensor(picked[:, 0], row(23), row(4), ALU.mult).then_inc(s_router, 1)
                if part == 14:
                    need(23)
                    dve.tensor_tensor(picked[:, 1], row(23), picked[:, 0], ALU.subtract)\
                        .then_inc(s_router, 1)

            def low(i, k):
                dve.wait_ge(s_hhi, at(i, K, k + 1))
                wait(dve, s_down, at(i, K, k + 1 - RING))
                dve.tensor_tensor(hlo[:, k % RING, :], hf[:, k % RING, :],
                                  hhi[:, k % RING, :].bitcast(F32), ALU.subtract).then_inc(s_hlo, 1)

            def weigh(i, par, e):
                dve.wait_ge(s_down, at(i, K, FC * (e + 1)))
                if isinstance(i, int) and i == 0:
                    if e * CBC_PARTS % E == 0:
                        dve.wait_ge(s_cbc_first[e * CBC_PARTS // E], 16)
                elif e == 0:
                    dve.wait_ge(s_cbc, at(i, 16, 0))
                if e == 0:
                    dst = acc[:, par, :]
                else:
                    wait(dve, s_acc, at(i, E - 1, e - 2) if e >= 2 else at(i, E - 1, 0))
                    dst = prod[:, e % 2, :]
                dve.tensor_tensor(dst, down[e % 2][:, :], cbc[:, par, e, :], ALU.mult).then_inc(s_prod, 1)

            def finish(i):
                dve.wait_ge(s_fin, at(i, 1, 1))
                dve.wait_ge(s_base, at(i, 16, 16))
                dve.wait_ge(s_z_stored, at(i, 16, 16))
                flat = res[:].rearrange("p t d -> p (t d)")
                dve.tensor_tensor(flat, pp[:, :], base[:].rearrange("p t d -> p (t d)"), ALU.add)\
                    .then_inc(s_fin_sum, 1)

            def ret_xlo(i, src):
                dve.wait_ge(s_xhi, at(i, 1, 1))
                dve.tensor_tensor(xlo[:], src[:, 0:T], xhi[:].bitcast(F32), ALU.subtract).then_inc(s_xlo, 1)

            def ret_low(i, src):
                dve.wait_ge(s_high, at(i, 1, 1))
                dve.tensor_tensor(split[:, 2, 0:T], src[:, 0:T], split[:, 0, 0:T].bitcast(F32), ALU.subtract)
                dve.tensor_tensor(split[:, 1, T:], src[:, T:], split[:, 0, T:].bitcast(F32), ALU.subtract)\
                    .then_inc(s_low, 1)

            def ret_k0_q1(i):
                dve.wait_ge(s_v_sb, at(i, V_COPIES, V_COPIES))
                wait(dve, s_av, at(i, TB, 0))
                dve.tensor_tensor(k0[:], pp[:, 0:P], const_of("kdecay_tok"), ALU.mult).then_inc(s_k0, 1)
                dve.tensor_tensor(q1[:], pp[:, 3 * P:4 * P], const_of("qdecay"), ALU.mult).then_inc(s_k0, 1)

            def ret_state(i):
                dve.wait_ge(s_state, at(i, 1, 1))
                dve.tensor_tensor(state[:], yy[:, T:T + P], const_of("headmask"), ALU.mult)\
                    .then_inc(s_state_sb, 1)

            def ret_mask(i, n):
                dve.wait_ge(s_score, at(i, TB * G, n + 1))
                t, g = n // G, n % G
                if isinstance(i, int) and i == 0 and n == 0:
                    dve.wait_ge(s_decay, 16)
                dve.tensor_tensor(A[t][:, g].rearrange("p h q -> p (h q)"), (m1, m0)[g % 2][:, :],
                                  const_of("decay")[:, g * GH * P:(g + 1) * GH * P], ALU.mult)\
                    .then_inc(s_A, 1)

            def ret_stats(i):
                dve.wait_ge(s_av, at(i, TB, TB))
                wait(dve, s_yn, at(i, 1, 0))
                dve.bn_stats(gst[:], yy[:, 0:T]).then_inc(s_gn_stats, 1)

            def ret_residual(i):
                dve.wait_ge(s_wo, at(i, 1, 1))
                dve.wait_ge(s_xres, at(i, 16, 16))
                wait(dve, s_xa_stored, at(i, 16, 0))
                dve.tensor_tensor(xa_out.rearrange("p t d -> p (t d)"), yy[:, T:2 * T],
                                  xres[:].rearrange("p t d -> p (t d)"), ALU.add).then_inc(s_wo_sb, 1)

            layernorm_stats(0, 0)
            layernorm_apply(0, 0)
            for n in range(WPROJ):
                weights(n)
            layernorm_stats(1, 0)
            dve.wait_ge(s_vecs, 16)
            prep_low(0, 0)
            weights(WPROJ)
            ret_xlo(0, m0)
            ret_low(0, m1)
            dve.wait_ge(s_const, 16)
            dve.wait_ge(s_vecs2, 32)

            def slot(i, par, first=False, norm=False, second=False, last=False):
                part = 0
                for k in range(K):
                    if first and k == 5:
                        layernorm_stats(2, par)
                    routing = not last and k >= ROUTER_AT and part < ROUTER_PARTS
                    if routing and k == ROUTER_AT:
                        prep_logits(i + 1)
                    low(i, k)
                    if routing:
                        router(i + 1, part)
                        part += 1
                    if first:
                        if k == 1:
                            prep_logits(0)
                            for n in range(ROUTER_PARTS):
                                router(0, n)
                        if k in DOWN_AT:
                            weights(WPROJ + 1 + DOWN_AT.index(k))
                    if k % 2 == 0:
                        if k >= 4:
                            weigh(i, par, (k - 4) // 2)
                        elif not first:
                            weigh(i - 1, 1 - par, E - 2 + k // 2)
                        if routing:
                            router(i + 1, part)
                            part += 1
                    if k == (2 if first else 1):
                        ret_k0_q1(i)
                    if k == 3 and not last:
                        prep_low(i + 1, 1 - par)
                    if k == 7 and not first:
                        ret_residual(i - 1)
                    if k == 11:
                        ret_state(i)
                    if k == 9 and not last:
                        ret_xlo(i + 1, yy)
                    if k == 12 and not last:
                        ret_low(i + 1, pp)
                    if SCORE_AT <= k < SCORE_AT + TB * G:
                        ret_mask(i, k - SCORE_AT)
                    if routing:
                        router(i + 1, part)
                        part += 1
                    if k == 9 and not first:
                        finish(i - 1)
                    if k == (14 if last else 15):
                        ret_stats(i)
                    if (first or norm) and k == (9 if first else 4):
                        layernorm_stats(3 if first else i + 3, par)
                if first:
                    dve.wait_ge(s_cbc_first[-1], 16)

            slots_of(dve, slot)
            weigh(SLOTS - 1, 1, E - 2)
            weigh(SLOTS - 1, 1, E - 1)
            ret_residual(B - 1)
            finish(SLOTS - 1)

        @block.gpsimd
        def _(pool):
            half = const_of("minus_half")
            pool.memset(vpad[:].rearrange("p t g h a d -> p (t g h a d)"), 0.0).then_inc(s_zero_wide, 1)
            pool.wait_ge(s_const0, 16)

            def layernorm(c):
                pool.wait_ge(s_ln_var, at(c, 1, 1))
                pool.wait_ge(s_ln_step, at(c, LN_OPS, LN_OPS))
                pool.tensor_tensor(ln[:, 0, :], ln[:, 4, :], half[:, 0:TI], ALU.pow).then_inc(s_ln_pow, 1)

            def layernorm_apply(c, par):
                x = buf_of(c, par)
                mean, rstd = (ln[:, n, :].unsqueeze(2).broadcast_to([P, TI, D]) for n in (5, 0))
                pool.wait_ge(s_ln_pow, at(c, 1, 1))
                pool.tensor_tensor(x, x, mean, ALU.subtract).then_inc(s_ln_centred, 1)
                pool.wait_ge(s_ln_centred, at(c, 1, 0))
                pool.tensor_tensor(x, x, rstd, ALU.mult).then_inc(s_ln, 1)

            def prep_norm(j):
                pool.wait_ge(s_sq, at(j, 1, 1))
                pool.tensor_tensor(ms[:, 1, :], ms[:, 0, :], const_of("over_d"), ALU.mult).then_inc(s_ms, 1)
                pool.wait_ge(s_ms, at(j, 2, 1))
                pool.tensor_tensor(ms[:, 2, :], ms[:, 1, :], const_of("rms_eps"), ALU.add).then_inc(s_ms, 1)
                pool.wait_ge(s_ms, at(j, 2, 2))
                pool.tensor_tensor(rstd[:], ms[:, 2, :], half[:, 0:TI], ALU.pow).then_inc(s_rstd, 1)
                pool.wait_ge(s_rstd, at(j, 1, 1))
                pool.tensor_tensor(zn[:], z_of(j), rstd[:].unsqueeze(2).broadcast_to([P, TI, D]), ALU.mult)\
                    .then_inc(s_zn, 1)

            def add(i, par, e):
                pool.wait_ge(s_prod, at(i, E, e + 1))
                if e > 1:
                    pool.wait_ge(s_acc, at(i, E - 1, e - 1))
                pool.tensor_tensor(acc[:, par, :], acc[:, par, :], prod[:, e % 2, :], ALU.add)\
                    .then_inc(s_acc, 1)

            def finish(i):
                pool.wait_ge(s_fin_sum, at(i, 1, 1))
                pool.wait_ge(s_xa_in, at(i - NI, 16, 16))
                if isinstance(i, int) and i == SLOTS - 1:
                    pool.wait_ge(s_wo_sb, B)
                    pool.tensor_tensor(res[:, 0:TB, :], res[:, 0:TB, :], xa_in[:, 0:TB, :], ALU.add)
                    pool.tensor_tensor(res[:, TB:, :], res[:, TB:, :], xa_out, ALU.add).then_inc(s_fin_out, 1)
                else:
                    pool.tensor_tensor(res[:], res[:], xa_in[:], ALU.add).then_inc(s_fin_out, 1)

            layernorm(0)
            prep_norm(0)
            layernorm(1)
            layernorm_apply(1, 0)

            def group_moments(i):
                def need(n):
                    pool.wait_ge(s_gn, at(i, GN_OPS, n))

                me, ve, mo, vo = gst[:, 1:2], gst[:, 2:3], gst[:, 4:5], gst[:, 5:6]
                pool.wait_ge(s_gn_stats, at(i, 1, 1))
                pool.tensor_tensor(gsq[:, 0:1], me, me, ALU.mult).then_inc(s_gn, 1)
                pool.tensor_tensor(gsq[:, 1:2], mo, mo, ALU.mult).then_inc(s_gn, 1)
                pool.tensor_scalar(gsq[:, 2:3], ve, vo, 2.0 / T, ALU.add, ALU.mult).then_inc(s_gn, 1)
                pool.tensor_tensor(ghm[:, 0:1], me, mo, ALU.add).then_inc(s_gn, 1)
                need(2)
                pool.tensor_tensor(gsq[:, 3:4], gsq[:, 0:1], gsq[:, 1:2], ALU.add).then_inc(s_gn, 1)
                need(5)
                pool.tensor_tensor(ghm[:, 1:2], gsq[:, 3:4], gsq[:, 2:3], ALU.add).then_inc(s_gn, 1)

            def group_affine(i):
                def need(n):
                    pool.wait_ge(s_gn, at(i, GN_OPS, n))

                pool.wait_ge(s_gn_mean, at(i, 1, 1))
                pool.tensor_tensor(gv[:, 0:1], gmv[:, 0:1], gmv[:, 0:1], ALU.mult).then_inc(s_gn, 1)
                pool.tensor_scalar(gv[:, 1:2], gmv[:, 1:2], LN_EPS, None, ALU.add).then_inc(s_gn, 1)
                need(8)
                pool.tensor_tensor(gv[:, 6:7], gv[:, 1:2], gv[:, 0:1], ALU.subtract).then_inc(s_gn, 1)
                need(9)
                pool.tensor_tensor(gv[:, 4:5], gv[:, 6:7], half[:, 0:1], ALU.pow).then_inc(s_gn, 1)
                need(10)
                pool.tensor_tensor(gv[:, 2:3], gv[:, 4:5], gnw_col, ALU.mult).then_inc(s_gn, 1)
                need(11)
                pool.tensor_tensor(gv[:, 5:6], gmv[:, 0:1], gv[:, 2:3], ALU.mult).then_inc(s_gn, 1)
                need(12)
                pool.tensor_tensor(gv[:, 3:4], gnb_col, gv[:, 5:6], ALU.subtract).then_inc(s_gn, 1)

            def spread_queries(i, g):
                pool.wait_ge(s_stack[g], at(i, 16 * COPIES, 16 * COPIES))
                if isinstance(i, int) and i == 0 and g == 0:
                    pool.wait_ge(s_const, 16)
                if g == 0:
                    wait(pool, s_score, at(i, TB * G, 0))
                pool.tensor_tensor(qblk[:, g], stack[:, g, 0:T].bitcast(F32).unsqueeze(1).broadcast_to([ROWS, GH, T]),
                                   const_of("blockmask")[0:ROWS].unsqueeze(2).broadcast_to([ROWS, GH, T]), ALU.mult)\
                    .then_inc(s_qblk, 1)

            def slot(i, par, first=False, norm=False, second=False, last=False):
                if not first:
                    add(i - 1, 1 - par, E - 2)
                if first:
                    prep_norm(1)
                spread_queries(i, 0)
                if not first:
                    add(i - 1, 1 - par, E - 1)
                    group_affine(i - 1)
                for g in range(1, G):
                    spread_queries(i, g)
                for e in range(1, E - 2):
                    if first and e == 1:
                        layernorm(2)
                        layernorm_apply(2, par)
                    if (first or norm) and e == (3 if first else 1):
                        layernorm(3 if first else i + 3)
                        layernorm_apply(3 if first else i + 3, par)
                    if second and e == 3:
                        finish(i - 1)
                    if e == E - 3 and not (isinstance(i, int) and i >= SLOTS - 2):
                        prep_norm(i + 2)
                    add(i, par, e)
                group_moments(i)

            slots_of(pool, slot, pairs_alone=1)
            group_affine(B - 1)
            add(SLOTS - 1, 1, E - 2)
            add(SLOTS - 1, 1, E - 1)
            finish(SLOTS - 1)


_INS = ["L0_attn_x", "L0_attn_W_q", "L0_attn_W_k", "L0_attn_W_v", "L0_attn_W_o", "L0_attn_gn_weight",
        "L0_attn_gn_bias", "L0_ffn_norm_w", "L0_ffn_w_macro", "L0_ffn_w_micro", "L0_ffn_w1", "L0_ffn_w2"]


def kernel(**inputs):
    import numpy as _np
    import concourse.bacc as _bacc
    from concourse import mybir as _mybir
    from concourse.bass_utils import run_bass_kernel_spmd as _run

    nc = _bacc.Bacc("TRN2", target_bir_lowering=False, num_devices=1)
    arrays, args = {}, []
    for name in _INS:
        a = _np.ascontiguousarray(inputs[name])
        arrays[f"in_{name}_dram"] = a
        args.append(nc.dram_tensor(f"in_{name}_dram", a.shape, _mybir.dt.from_np(a.dtype), kind="ExternalInput").ap())
    arrays["constants_dram"] = constants()
    args.append(nc.dram_tensor("constants_dram", (P, NCONST), F32, kind="ExternalInput").ap())
    args.append(nc.dram_tensor("out_0_dram", (B, T, D), F32, kind="ExternalOutput").ap())
    program(nc, *args)
    r = _run(nc, [arrays], core_ids=[0])
    return r.results[0]["out_0_dram"]
```
